# Optimizing a Trainium2 kernel written in Bass

```python
import numpy as np
import jax
import jax.numpy as jnp

def _softmax(x, axis=-1):
    return jax.nn.softmax(x, axis=axis)

def _gelu(x):
    return jax.nn.gelu(x, approximate=True)

def _silu(x):
    return jax.nn.silu(x)

def _sigmoid(x):
    return jax.nn.sigmoid(x)

def _layernorm(x, axis=-1, eps=1e-05):
    m = jnp.mean(x, axis=axis, keepdims=True)
    v = jnp.var(x, axis=axis, keepdims=True)
    return (x - m) / jnp.sqrt(v + eps)

def _scatter_add(tgt, idx, src, axis=0):
    return tgt.at[idx].add(src)

def _segment_sum(src, seg, n):
    return jax.ops.segment_sum(src, seg, n)
kernel_name = 'mk_adj_preln_d1_adj_r2_506873'

def setup_inputs(seed: int=0):
    np.random.seed(seed)
    _w = jnp.asarray

    def _rec_inputs():
        import jax
        import jax.numpy as jnp
        _gk = jax.random.key(seed)
        x = -0.000125 + 0.9999 * jax.random.normal(jax.random.fold_in(_gk, 1), (64, 128, 512), jnp.float32)
        _w = (1.0 + jnp.arange(128, dtype=jnp.float32)) ** (-0.5)
        _w = _w / _w.mean()
        _pij = jnp.clip(0.03125 * _w[:, None] * _w[None, :], 0.0, 1.0)
        _a = jax.random.uniform(jax.random.fold_in(_gk, 2), (128, 128)) < _pij
        adj = _a.astype(jnp.int32)
        return (x, adj)
    x, adj = _rec_inputs()

    def _L0_gnn_setup():
        import jax, jax.numpy as jnp
        import numpy as np
        B, N, E, H = (64, 256, 512, 16)
        DH = E // H
        key = jax.random.key(seed)
        ks = jax.random.split(key, 5)
        x = jax.random.normal(ks[0], (B, N, E), dtype=jnp.float32)
        Wqkv = jax.random.normal(ks[1], (E, 3 * E), dtype=jnp.float32) * 0.02
        bqkv = jnp.zeros((3 * E,), dtype=jnp.float32)
        Wproj = jax.random.normal(ks[2], (E, E), dtype=jnp.float32) * 0.02
        bproj = jnp.zeros((E,), dtype=jnp.float32)
        adj = jax.random.randint(ks[3], (N, N), 0, 2, dtype=jnp.int32)
        return {'x': x, 'Wqkv': Wqkv, 'bqkv': bqkv, 'Wproj': Wproj, 'bproj': bproj, 'adj': adj}
    _L0_gnn_all = _L0_gnn_setup()
    _L0_gnn_in = {k: v for k, v in _L0_gnn_all.items() if k in ('Wqkv', 'bqkv', 'Wproj', 'bproj')}
    del _L0_gnn_all
    return {'x': x, 'adj': adj, 'L0_gnn_Wqkv': _L0_gnn_in['Wqkv'], 'L0_gnn_bqkv': _L0_gnn_in['bqkv'], 'L0_gnn_Wproj': _L0_gnn_in['Wproj'], 'L0_gnn_bproj': _L0_gnn_in['bproj']}

def reference(x, adj, L0_gnn_Wqkv, L0_gnn_bqkv, L0_gnn_Wproj, L0_gnn_bproj):
    import jax
    import jax.numpy as jnp

    def _L0_gnn_ref(x, Wqkv, bqkv, Wproj, bproj, adj):
        import jax, jax.numpy as jnp
        import numpy as np
        B, N, E, H = (64, 256, 512, 16)
        DH = E // H
        b, n, e = x.shape
        h, dh = (H, e // H)
        qkv = (x @ Wqkv + bqkv).reshape(b, n, 3, h, dh)
        qkv = jnp.transpose(qkv, (2, 0, 3, 1, 4))
        q, k, v = (qkv[0], qkv[1], qkv[2])
        mask = adj + jnp.eye(n, dtype=adj.dtype) > 0
        scale = 1.0 / jnp.sqrt(jnp.asarray(dh, dtype=x.dtype))
        scores = jnp.einsum('bhnd,bhmd->bhnm', q, k) * scale
        scores = jnp.where(mask[None, None], scores, jnp.finfo(scores.dtype).min)
        attn = jax.nn.softmax(scores, axis=-1)
        y = jnp.einsum('bhnm,bhmd->bhnd', attn, v)
        y = jnp.transpose(y, (0, 2, 1, 3)).reshape(b, n, e)
        return y @ Wproj + bproj
    h = jnp.maximum(_layernorm(x, axis=-1), 0.0)
    x = x + _L0_gnn_ref(h, L0_gnn_Wqkv, L0_gnn_bqkv, L0_gnn_Wproj, L0_gnn_bproj, adj)
    return x

_drawn_inputs = setup_inputs


def setup_inputs(seed=0):
    import zlib

    import numpy as np

    out = dict(_drawn_inputs(seed))
    spreads = {'L0_gnn_bqkv': (0.0, 0.1), 'L0_gnn_bproj': (0.0, 0.1)}
    factors = {}
    for name, (base, spread) in spreads.items():
        noise = np.random.default_rng([zlib.crc32(name.encode()), seed]).standard_normal(out[name].shape)
        drawn = base * np.exp(spread * noise) if base else spread * noise
        out[name] = jnp.asarray(drawn.astype(out[name].dtype))
    for name, factor in factors.items():
        out[name] = (out[name] * factor).astype(out[name].dtype)
    return out
```

```python
from contextlib import ExitStack

import concourse.bass as bass
from concourse import mybir

F32 = mybir.dt.float32
F32R = mybir.dt.float32r
I32 = mybir.dt.int32
ALU = mybir.AluOpType
ACT = mybir.ActivationFunctionType
AX_X = mybir.AxisListType.X

P = 128
HEADS = 16
EPS = 1e-5
MASKED = -(2.0 ** 126)
GROUP = 4
QUADRANT = 32
UNROLL = 2


def wait(engine, semaphore, value):
    if isinstance(value, int) and value <= 0:
        return
    engine.wait_ge(semaphore, value)


def graph_attention_block(nc, x, adj, w_qkv, b_qk_columns, b_v, w_proj, b_proj, out):
    BATCHES, N, E = x.shape
    GROUPS = BATCHES // GROUP
    CHUNKS = E // P
    HPC = HEADS // CHUNKS
    DH = E // HEADS
    SCALE = float(DH) ** -0.5
    assert N == P and DH == QUADRANT and CHUNKS == GROUP and GROUPS % UNROLL == 0

    with ExitStack() as ctx:
        def sb(name, shape, dt=F32):
            return ctx.enter_context(nc.sbuf_tensor(name, shape, dt))

        def bank(name):
            return ctx.enter_context(nc.psum_tensor(name, [P, 512], F32))

        def sem(name):
            return ctx.enter_context(nc.semaphore(name))

        wqkv_hi = sb("wqkv_hi", [P, CHUNKS, 3 * E], F32R)
        wqkv_lo = sb("wqkv_lo", [P, CHUNKS, 3 * E], F32R)
        wproj_hi = sb("wproj_hi", [P, CHUNKS, E], F32R)
        wproj_lo = sb("wproj_lo", [P, CHUNKS, E], F32R)
        bqk = sb("bqk", [P, 2 * CHUNKS])
        bv_rows = sb("bv_rows", [P, E])
        bproj_rows = sb("bproj_rows", [P, E])
        identity = sb("identity", [P, P])
        mask_bias = sb("mask_bias", [P, P])
        minus_half = sb("minus_half", [P, 1])
        x_in = sb("x_in", [P, 2, E])
        stats = sb("stats", [P, 6])
        mean_var = sb("mean_var", [P, 2, 2])
        var_eps = sb("var_eps", [P, 2, 1])
        rstd = sb("rstd", [P, 2, 1])
        normed = sb("normed", [P, E])
        ht_hi = sb("ht_hi", [P, 2, CHUNKS, GROUP * N], F32R)
        ht_lo = sb("ht_lo", [P, 2, CHUNKS, GROUP * N], F32R)
        qt_hi = sb("qt_hi", [P, 2, CHUNKS, GROUP * N], F32R)
        qt_lo = sb("qt_lo", [P, 2, CHUNKS, GROUP * N], F32R)
        kt = sb("kt", [P, 2, CHUNKS, GROUP * N])
        v = sb("v", [P, 2 * GROUP, E])
        kdiag_hi = sb("kdiag_hi", [P, CHUNKS, HPC * N], F32R)
        kdiag_lo = sb("kdiag_lo", [P, CHUNKS, HPC * N], F32R)
        probs = sb("probs", [P, CHUNKS, HPC * N])
        row_max = sb("row_max", [P, HEADS])
        neg_max = sb("neg_max", [P, HEADS])
        row_sum = sb("row_sum", [P, HEADS])
        inv_sum = sb("inv_sum", [P, HEADS])
        pt = sb("pt", [P, 2, HPC * N])
        yt_hi = sb("yt_hi", [P, CHUNKS, N], F32R)
        yt_lo = sb("yt_lo", [P, CHUNKS, N], F32R)
        residual = sb("residual", [P, 2, E])

        ps_scores = [bank("ps_scores0"), bank("ps_scores1")]
        ps_pt = [bank("ps_pt0"), bank("ps_pt1")]
        ps_qk = bank("ps_qk")
        ps_vo = bank("ps_vo")
        ps_ht = bank("ps_ht")
        ps_yt = bank("ps_yt")

        x_loaded = [sem("x_loaded0"), sem("x_loaded1")]
        res_loaded = [sem("res_loaded0"), sem("res_loaded1")]
        stored = [sem("stored0"), sem("stored1")]
        consts_loaded = sem("consts_loaded")
        wqkv_loaded = sem("wqkv_loaded")
        wproj_loaded = sem("wproj_loaded")
        zeroed = sem("zeroed")
        identity_ready = sem("identity_ready")
        mask_step = sem("mask_step")
        w_hi_ready = sem("w_hi_ready")
        wqkv_ready = sem("wqkv_ready")
        wproj_ready = sem("wproj_ready")
        stats_ready = sem("stats_ready")
        moments_ready = sem("moments_ready")
        eps_added = sem("eps_added")
        rstd_ready = sem("rstd_ready")
        normed_ready = sem("normed_ready")
        ht_in_psum = sem("ht_in_psum")
        ht_hi_ready = sem("ht_hi_ready")
        ht_ready = sem("ht_ready")
        k_in_psum = sem("k_in_psum")
        kt_ready = sem("kt_ready")
        q_in_psum = sem("q_in_psum")
        q_hi_ready = sem("q_hi_ready")
        q_ready = sem("q_ready")
        v_in_psum = sem("v_in_psum")
        v_ready = sem("v_ready")
        kdiag_hi_ready = sem("kdiag_hi_ready")
        kdiag_ready = sem("kdiag_ready")
        scores_in_psum = sem("scores_in_psum")
        scores_masked = sem("scores_masked")
        max_ready = sem("max_ready")
        neg_max_ready = sem("neg_max_ready")
        exp_ready = sem("exp_ready")
        inv_sum_ready = sem("inv_sum_ready")
        probs_ready = sem("probs_ready")
        pt_in_psum = sem("pt_in_psum")
        pt_ready = sem("pt_ready")
        pv_done = sem("pv_done")
        yt_hi_ready = sem("yt_hi_ready")
        yt_ready = sem("yt_ready")
        proj_in_psum = sem("proj_in_psum")
        res_biased = sem("res_biased")
        out_ready = sem("out_ready")

        def wqkv_stage(k):
            flat = kt if k < 2 else v
            flat = flat[:, :, :, :].rearrange("p a c n -> p (a c n)") if k < 2 else flat[:, :, :].rearrange("p b e -> p (b e)")
            return flat[:, (k % 2) * 3 * E:(k % 2 + 1) * 3 * E]

        wproj_stage = probs
        adj_int = pt[:, 0, 0:P].bitcast(I32)

        def by_head(tile):
            return tile.rearrange("p (h n) -> p h n", h=HPC)

        def pipeline(engine, step):
            first, last = 3, GROUPS - 1
            turns = (last - first + 1) // UNROLL
            for i in range(first):
                for t in range(GROUP):
                    step(i, t, i % 2, i < GROUPS, 1 <= i, 2 <= i, i == 2 and t == 0)
            with engine.Fori(first, first + turns * UNROLL, UNROLL) as base:
                for u in range(UNROLL):
                    for t in range(GROUP):
                        step(base + u, t, (first + u) % 2, True, True, True, False)
            for i in range(first + turns * UNROLL, GROUPS + 2):
                for t in range(GROUP):
                    step(i, t, i % 2, i < GROUPS, i <= GROUPS, True, False)

        def has_next(i, t):
            return not isinstance(i, int) or 0 <= 4 * (i - 2) + t + 1 < BATCHES

        block = ctx.enter_context(nc.Block())

        @block.sync
        def _(sp):
            def load_x(f, slot, uses):
                wait(sp, normed_ready, f - 1)
                sp.dma_start(x_in[:, slot, :], x[bass.ds(f, 1)].rearrange("b n e -> (b n) e")).then_inc(x_loaded[slot], 16)

            def store(b, slot):
                sp.wait_ge(out_ready, b + 1)
                sp.dma_start(out[bass.ds(b, 1)].rearrange("b n e -> (b n) e"), residual[:, slot, :]).then_inc(stored[slot], 16)

            load_x(0, 0, 0)
            load_x(1, 1, 0)
            sp.dma_start(adj_int, adj).then_inc(consts_loaded, 16)
            sp.dma_start(bqk[:, :], b_qk_columns).then_inc(consts_loaded, 16)
            sp.dma_start(bv_rows[:, :], b_v.to_broadcast([P, E])).then_inc(consts_loaded, 16)
            sp.dma_start(bproj_rows[:, :], b_proj.to_broadcast([P, E])).then_inc(consts_loaded, 16)
            for k in range(CHUNKS):
                sp.dma_start(wqkv_stage(k), w_qkv[k * P:(k + 1) * P, :]).then_inc(wqkv_loaded, 16)
            sp.dma_start(wproj_stage[:, :, :], w_proj.rearrange("(k p) n -> p k n", p=P)).then_inc(wproj_loaded, 16)

            def step(i, t, par, front, middle, attention, opening):
                slot = t % 2
                if front and not (isinstance(i, int) and i == 0 and t < 2):
                    load_x(4 * i + t, slot, 0)
                if attention:
                    a = 4 * (i - 2) + t
                    earlier = isinstance(i, int) and i == 2 and t < 2
                    if not earlier:
                        store(a - 2, slot)
                        sp.wait_ge(stored[slot], 16 * (2 * (i - 2) + t // 2))
                    sp.dma_start(residual[:, slot, :], x[bass.ds(a, 1)].rearrange("b n e -> (b n) e")).then_inc(res_loaded[slot], 16)

            pipeline(sp, step)
            for b in (BATCHES - 2, BATCHES - 1):
                store(b, b % 2)
            for slot in range(2):
                sp.wait_ge(stored[slot], 16 * (BATCHES // 2))

        @block.gpsimd
        def _(pool):
            nc.gpsimd.memset(identity[:, :], 0.0).then_inc(zeroed, 1)
            nc.gpsimd.memset(minus_half[:, :], -0.5).then_inc(zeroed, 1)
            pool.wait_ge(zeroed, 2)
            nc.gpsimd.affine_select(out=identity[:, :], in_=identity[:, :], compare_op=ALU.not_equal, fill=1.0, base=0,
                                    pattern=[[-1, P]], channel_multiplier=1).then_inc(identity_ready, 1)
            nc.gpsimd.memset(kdiag_hi[:, :, :].bitcast(F32), 0.0).then_inc(zeroed, 1)
            nc.gpsimd.memset(kdiag_lo[:, :, :].bitcast(F32), 0.0).then_inc(zeroed, 1)

            def inverse_std(f, slot):
                pool.wait_ge(eps_added, f + 1)
                nc.gpsimd.tensor_tensor(rstd[:, slot, :], var_eps[:, slot, :], minus_half[:, :], ALU.pow).then_inc(rstd_ready, 1)

            def normalise_probs(a, c):
                pool.wait_ge(inv_sum_ready, 4 * a + c + 1)
                heads = slice(HPC * c, HPC * (c + 1))
                nc.gpsimd.tensor_tensor(by_head(probs[:, c, :]), by_head(probs[:, c, :]),
                                        inv_sum[:, heads].unsqueeze(2).to_broadcast([P, HPC, N]),
                                        ALU.mult).then_inc(probs_ready, 1)

            def step(i, t, par, front, middle, attention, opening):
                a = 4 * (i - 2) + t
                if attention:
                    slot = t % 2
                    pool.wait_ge(res_loaded[slot], 16 * (2 * (i - 2) + t // 2 + 1))
                    pool.wait_ge(consts_loaded, 64)
                    nc.gpsimd.tensor_tensor(residual[:, slot, :], residual[:, slot, :], bproj_rows[:, :],
                                            ALU.add).then_inc(res_biased, 1)
                    normalise_probs(a, 0)
                if front:
                    inverse_std(4 * i + t, t % 2)
                if attention:
                    normalise_probs(a, 1)
                    normalise_probs(a, 2)
                    normalise_probs(a, 3)

            pipeline(pool, step)

        @block.scalar
        def _(act):
            act.wait_ge(wqkv_loaded, 16 * CHUNKS)
            for k in range(CHUNKS):
                nc.scalar.activation(wqkv_hi[:, k, :], wqkv_stage(k), ACT.Copy).then_inc(w_hi_ready, 1)
            act.wait_ge(wproj_loaded, 16)
            nc.scalar.activation(wproj_hi[:, :, :], wproj_stage[:, :, :], ACT.Copy).then_inc(w_hi_ready, 1)
            act.wait_ge(consts_loaded, 64)

            def exp_chunk(a, c):
                act.wait_ge(neg_max_ready, 4 * a + c + 1)
                for h in range(HPC * c, HPC * (c + 1)):
                    tile = probs[:, c, N * (h % HPC):N * (h % HPC + 1)]
                    last = nc.scalar.activation(tile, tile, ACT.Exp, bias=neg_max[:, h:h + 1], accum_out=row_sum[:, h:h + 1])
                last.then_inc(exp_ready, 1)

            def pt_chunk(a, c):
                act.wait_ge(pt_in_psum, 4 * a + c + 1)
                wait(act, pv_done, 4 * a + c - 1)
                nc.scalar.activation(pt[:, c % 2, :], ps_pt[c % 2][:, :], ACT.Copy).then_inc(pt_ready, 1)

            def step(i, t, par, front, middle, attention, opening):
                f, m, a = 4 * i + t, 4 * (i - 1) + t, 4 * (i - 2) + t
                if attention:
                    exp_chunk(a, 0)
                if middle:
                    act.wait_ge(k_in_psum, m + 1)
                    wait(act, kdiag_ready, 16 * (i - 2))
                    nc.scalar.activation(kt[:, 1 - par, t, :], ps_qk[:, :], ACT.Identity,
                                         bias=bqk[:, CHUNKS + t:CHUNKS + t + 1]).then_inc(kt_ready, 1)
                if attention:
                    exp_chunk(a, 1)
                    exp_chunk(a, 2)
                    exp_chunk(a, 3)
                    pt_chunk(a, 0)
                if middle:
                    act.wait_ge(q_in_psum, m + 1)
                    wait(act, scores_in_psum, 16 * (i - 2))
                    nc.scalar.activation(qt_hi[:, 1 - par, t, :], ps_qk[:, :], ACT.Identity,
                                         bias=bqk[:, t:t + 1]).then_inc(q_hi_ready, 1)
                if attention:
                    pt_chunk(a, 1)
                    pt_chunk(a, 2)
                    pt_chunk(a, 3)
                if front:
                    act.wait_ge(ht_in_psum, f + 1)
                    wait(act, v_in_psum, 4 * (i - 1))
                    nc.scalar.activation(ht_hi[:, par, :, N * t:N * (t + 1)], ps_ht[:, :].rearrange("p (k n) -> p k n", k=CHUNKS),
                                         ACT.Relu).then_inc(ht_hi_ready, 1)
                if attention:
                    act.wait_ge(pv_done, 4 * (a + 1))
                    wait(act, proj_in_psum, a)
                    nc.scalar.activation(yt_hi[:, :, :], ps_yt[:, :].rearrange("p (c n) -> p c n", c=CHUNKS),
                                         ACT.Copy).then_inc(yt_hi_ready, 1)

            pipeline(act, step)

        @block.vector
        def _(dve):
            def row_stats(slot, loads):
                dve.wait_ge(x_loaded[slot], 16 * loads)
                nc.vector.bn_stats(stats[:, :], x_in[:, slot, :]).then_inc(stats_ready, 1)

            def moments(f, slot):
                nc.vector.bn_aggr(mean_var[:, slot, :], stats[:, :]).then_inc(moments_ready, 1)
                dve.wait_ge(moments_ready, f + 1)
                nc.vector.tensor_scalar(var_eps[:, slot, :], mean_var[:, slot, 1:2], EPS, None, ALU.add).then_inc(eps_added, 1)

            def normalise(f, slot):
                dve.wait_ge(rstd_ready, f + 1)
                wait(dve, ht_in_psum, f)
                nc.vector.tensor_scalar(normed[:, :], x_in[:, slot, :], mean_var[:, slot, 0:1], rstd[:, slot, :],
                                        ALU.subtract, ALU.mult).then_inc(normed_ready, 1)

            def split_qkv():
                for k in range(CHUNKS):
                    dve.wait_ge(w_hi_ready, k + 1)
                    last = nc.vector.tensor_tensor(wqkv_lo[:, k, :], wqkv_stage(k), wqkv_hi[:, k, :].bitcast(F32), ALU.subtract)
                last.then_inc(wqkv_ready, 1)

            def split_proj():
                dve.wait_ge(w_hi_ready, CHUNKS + 1)
                nc.vector.tensor_tensor(wproj_lo[:, :, :], wproj_stage[:, :, :], wproj_hi[:, :, :].bitcast(F32),
                                        ALU.subtract).then_inc(wproj_ready, 1)

            def make_mask():
                dve.wait_ge(consts_loaded, 64)
                dve.wait_ge(identity_ready, 1)
                nc.vector.tensor_tensor(mask_bias[:, :], adj_int, identity[:, :], ALU.add).then_inc(mask_step, 1)
                dve.wait_ge(mask_step, 1)
                nc.vector.tensor_scalar(mask_bias[:, :], mask_bias[:, :], 0.0, None, ALU.is_gt).then_inc(mask_step, 1)
                dve.wait_ge(mask_step, 2)
                nc.vector.tensor_scalar(mask_bias[:, :], mask_bias[:, :], 1.0, -MASKED, ALU.subtract, ALU.mult).then_inc(mask_step, 1)
                dve.wait_ge(mask_step, 3)

            def masked_max(a, c):
                dve.wait_ge(scores_in_psum, 4 * a + c + 1)
                wait(dve, pt_in_psum, 4 * a + c - 3)
                nc.vector.scalar_tensor_tensor(out=by_head(probs[:, c, :]), in0=by_head(ps_scores[c % 2][:, :]), scalar=SCALE,
                                               in1=mask_bias[:, :].unsqueeze(1).to_broadcast([P, HPC, N]),
                                               op0=ALU.mult, op1=ALU.add).then_inc(scores_masked, 1)
                heads = slice(HPC * c, HPC * (c + 1))
                dve.wait_ge(scores_masked, 4 * a + c + 1)
                nc.vector.tensor_reduce(row_max[:, heads], by_head(probs[:, c, :]), AX_X, ALU.max).then_inc(max_ready, 1)
                dve.wait_ge(max_ready, 4 * a + c + 1)
                nc.vector.tensor_scalar(neg_max[:, heads], row_max[:, heads], -1.0, None, ALU.mult).then_inc(neg_max_ready, 1)

            def invert_sum(a, c):
                heads = slice(HPC * c, HPC * (c + 1))
                dve.wait_ge(exp_ready, 4 * a + c + 1)
                nc.vector.reciprocal(inv_sum[:, heads], row_sum[:, heads]).then_inc(inv_sum_ready, 1)

            def step(i, t, par, front, middle, attention, opening):
                f, m, a = 4 * i + t, 4 * (i - 1) + t, 4 * (i - 2) + t
                if attention:
                    masked_max(a, 0)
                if front:
                    row_stats(t % 2, 2 * i + t // 2 + 1)
                if attention:
                    masked_max(a, 1)
                if front:
                    dve.wait_ge(stats_ready, f + 1)
                if attention:
                    invert_sum(a, 0)
                if front:
                    moments(f, t % 2)
                if attention:
                    masked_max(a, 2)
                    invert_sum(a, 1)
                    masked_max(a, 3)
                    invert_sum(a, 2)
                if has_next(i, t):
                    nxt, npar, nt = (a + 1, par if t < 3 else 1 - par, (t + 1) % GROUP)
                    dve.wait_ge(kt_ready, group_steps(i, t))
                    if attention:
                        dve.wait_ge(scores_in_psum, 4 * (a + 1))
                    dve.wait_ge(zeroed, 4)
                    for j in range(HPC):
                        rows = slice(QUADRANT * j, QUADRANT * (j + 1))
                        nc.vector.tensor_copy(kdiag_hi[rows, :, N * j:N * (j + 1)],
                                              kt[rows, npar, :, N * nt:N * (nt + 1)]).then_inc(kdiag_hi_ready, 1)
                if attention and not opening:
                    add_residual(a - 1, (t - 1) % 2)
                if has_next(i, t):
                    for j in range(HPC):
                        rows = slice(QUADRANT * j, QUADRANT * (j + 1))
                        dve.wait_ge(kdiag_hi_ready, 4 * nxt + j + 1)
                        nc.vector.tensor_tensor(kdiag_lo[rows, :, N * j:N * (j + 1)], kt[rows, npar, :, N * nt:N * (nt + 1)],
                                                kdiag_hi[rows, :, N * j:N * (j + 1)].bitcast(F32),
                                                ALU.subtract).then_inc(kdiag_ready, 1)
                if attention:
                    invert_sum(a, 3)
                if front:
                    normalise(f, t % 2)
                if middle:
                    dve.wait_ge(q_hi_ready, m + 1)
                    nc.vector.scalar_tensor_tensor(out=qt_lo[:, 1 - par, t, :], in0=ps_qk[:, :], scalar=bqk[:, t:t + 1],
                                                   in1=qt_hi[:, 1 - par, t, :].bitcast(F32),
                                                   op0=ALU.add, op1=ALU.subtract).then_inc(q_ready, 1)
                    dve.wait_ge(v_in_psum, m + 1)
                    wait(dve, pv_done, 16 * (i - 2))
                    nc.vector.tensor_tensor(v[:, GROUP * (1 - par) + t, :], ps_vo[:, :], bv_rows[:, :], ALU.add).then_inc(v_ready, 1)
                if front:
                    dve.wait_ge(ht_hi_ready, f + 1)
                    nc.vector.scalar_tensor_tensor(out=ht_lo[:, par, :, N * t:N * (t + 1)],
                                                   in0=ps_ht[:, :].rearrange("p (k n) -> p k n", k=CHUNKS), scalar=0.0,
                                                   in1=ht_hi[:, par, :, N * t:N * (t + 1)].bitcast(F32),
                                                   op0=ALU.max, op1=ALU.subtract).then_inc(ht_ready, 1)
                if attention:
                    dve.wait_ge(yt_hi_ready, a + 1)
                    nc.vector.tensor_tensor(yt_lo[:, :, :], ps_yt[:, :].rearrange("p (c n) -> p c n", c=CHUNKS),
                                            yt_hi[:, :, :].bitcast(F32), ALU.subtract).then_inc(yt_ready, 1)
                if isinstance(i, int) and i == 0 and t == 0:
                    make_mask()
                    split_qkv()
                    split_proj()

            def group_steps(i, t):
                return 4 * (i - 1) if t < GROUP - 1 else 4 * i

            def add_residual(b, slot):
                dve.wait_ge(proj_in_psum, b + 1)
                dve.wait_ge(res_biased, b + 1)
                nc.vector.tensor_tensor(residual[:, slot, :], ps_vo[:, :], residual[:, slot, :], ALU.add).then_inc(out_ready, 1)

            pipeline(dve, step)
            add_residual(BATCHES - 1, (BATCHES - 1) % 2)

        @block.tensor
        def _(pe):
            pe.wait_ge(identity_ready, 1)

            def three_passes(out_tile, stationary, moving, ks, first, last):
                (s_hi, s_lo), (m_hi, m_lo) = stationary, moving
                for k in ks:
                    for n, (s, m) in enumerate(((s_hi, m_hi), (s_hi, m_lo), (s_lo, m_hi))):
                        done = nc.tensor.matmul(out_tile, s(k), m(k), start=(first and k == ks[0] and n == 0),
                                                stop=(last and k == ks[-1] and n == 2))
                return done

            def projection(out_tile, stationary, moving, half):
                ks = list(range(CHUNKS // 2)) if half == 0 else list(range(CHUNKS // 2, CHUNKS))
                return three_passes(out_tile, stationary, moving, ks, half == 0, half == 1)

            def parts(hi, lo, at):
                return (lambda k: at(hi, k)), (lambda k: at(lo, k))

            def qk_half(i, t, par, offset, half):
                return projection(ps_qk[:, :],
                                  parts(wqkv_hi, wqkv_lo, lambda w, k: w[:, k, offset + P * t:offset + P * (t + 1)]),
                                  parts(ht_hi, ht_lo, lambda h, k: h[:, 1 - par, k, :]), half)

            def k_half(i, t, par, half):
                m = 4 * (i - 1) + t
                if half == 0:
                    if t == 0:
                        pe.wait_ge(wqkv_ready, 1)
                        pe.wait_ge(ht_ready, 4 * i)
                    wait(pe, q_ready, m)
                done = qk_half(i, t, par, E, half)
                if half == 1:
                    done.then_inc(k_in_psum, 1)

            def q_half(i, t, par, half):
                m = 4 * (i - 1) + t
                if half == 0:
                    pe.wait_ge(kt_ready, m + 1)
                done = qk_half(i, t, par, 0, half)
                if half == 1:
                    done.then_inc(q_in_psum, 1)

            def v_half(i, t, par, half, after_projection):
                if half == 0 and after_projection:
                    pe.wait_ge(out_ready, 4 * (i - 2) + t)
                elif half == 0:
                    wait(pe, v_ready, 4 * (i - 1) + t)
                done = projection(ps_vo[:, :],
                                  parts(ht_hi, ht_lo, lambda h, k: h[:, 1 - par, k, N * t:N * (t + 1)]),
                                  parts(wqkv_hi, wqkv_lo, lambda w, k: w[:, k, 2 * E:3 * E]), half)
                if half == 1:
                    done.then_inc(v_in_psum, 1)

            def proj_half(b, vs, half):
                if half == 0:
                    pe.wait_ge(wproj_ready, 1)
                    pe.wait_ge(yt_ready, b + 1)
                    pe.wait_ge(v_ready, vs)
                done = projection(ps_vo[:, :], parts(yt_hi, yt_lo, lambda y, k: y[:, k, :]),
                                  parts(wproj_hi, wproj_lo, lambda w, k: w[:, k, :]), half)
                if half == 1:
                    done.then_inc(proj_in_psum, 1)

            def scores(i, t, par, c):
                a = 4 * (i - 2) + t
                if c == 0:
                    pe.wait_ge(kdiag_ready, 4 * (a + 1))
                    if t == 0:
                        pe.wait_ge(q_ready, 4 * (i - 1))
                wait(pe, scores_masked, 4 * a + c - 1)
                three_passes(ps_scores[c % 2][:, :],
                             parts(qt_hi, qt_lo, lambda q, _: q[:, par, c, N * t:N * (t + 1)]),
                             parts(kdiag_hi, kdiag_lo, lambda k, _: k[:, c, :]), [0], True, True).then_inc(scores_in_psum, 1)

            def transpose_probs(a, c):
                pe.wait_ge(probs_ready, 4 * a + c + 1)
                wait(pe, pt_ready, 4 * a + c - 1)
                for j in range(HPC):
                    last = nc.tensor.transpose(ps_pt[c % 2][:, N * j:N * (j + 1)], probs[:, c, N * j:N * (j + 1)], identity[:, :])
                last.then_inc(pt_in_psum, 1)

            def pv(i, t, par, c):
                a = 4 * (i - 2) + t
                if c == 0:
                    pe.wait_ge(v_ready, a + 1)
                    wait(pe, yt_ready, a)
                pe.wait_ge(pt_ready, 4 * a + c + 1)
                for j in range(HPC):
                    h = HPC * c + j
                    last = nc.tensor.matmul(ps_yt[QUADRANT * j:QUADRANT * (j + 1), N * c:N * (c + 1)],
                                            v[:, GROUP * par + t, DH * h:DH * (h + 1)],
                                            pt[:, c % 2, N * j:N * (j + 1)], start=True, stop=True)
                last.then_inc(pv_done, 1)

            def transpose_rows(f):
                pe.wait_ge(normed_ready, f + 1)
                wait(pe, ht_ready, f)
                for k in range(CHUNKS):
                    last = nc.tensor.transpose(ps_ht[:, N * k:N * (k + 1)], normed[:, P * k:P * (k + 1)], identity[:, :])
                last.then_inc(ht_in_psum, 1)

            def step(i, t, par, front, middle, attention, opening):
                f, a = 4 * i + t, 4 * (i - 2) + t
                v_steps = 4 * (i - 1) + t
                if not middle or (isinstance(i, int) and i > GROUPS):
                    v_steps = BATCHES
                if attention:
                    scores(i, t, par, 0)
                if middle:
                    k_half(i, t, par, 0)
                if attention:
                    scores(i, t, par, 1)
                if middle:
                    k_half(i, t, par, 1)
                if attention:
                    scores(i, t, par, 2)
                    if not opening:
                        proj_half(a - 1, v_steps, 0)
                    scores(i, t, par, 3)
                    if not opening:
                        proj_half(a - 1, v_steps, 1)
                if middle:
                    q_half(i, t, par, 0)
                if attention:
                    transpose_probs(a, 0)
                if middle:
                    q_half(i, t, par, 1)
                if attention:
                    transpose_probs(a, 1)
                if middle:
                    v_half(i, t, par, 0, attention and not opening)
                if attention:
                    transpose_probs(a, 2)
                    pv(i, t, par, 0)
                if middle:
                    v_half(i, t, par, 1, attention and not opening)
                if attention:
                    transpose_probs(a, 3)
                    pv(i, t, par, 1)
                if front:
                    transpose_rows(f)
                if attention:
                    pv(i, t, par, 2)
                    pv(i, t, par, 3)

            pipeline(pe, step)
            proj_half(BATCHES - 1, BATCHES, 0)
            proj_half(BATCHES - 1, BATCHES, 1)


def kernel(x, adj, L0_gnn_Wqkv, L0_gnn_bqkv, L0_gnn_Wproj, L0_gnn_bproj):
    import numpy as np
    import concourse.bacc as bacc
    from concourse.bass_utils import run_bass_kernel_spmd

    e = L0_gnn_Wproj.shape[0]
    bqkv = np.asarray(L0_gnn_bqkv)
    arrays = {
        "x": np.ascontiguousarray(x),
        "adj": np.ascontiguousarray(adj),
        "w_qkv": np.ascontiguousarray(L0_gnn_Wqkv),
        "b_qk_columns": np.ascontiguousarray(bqkv[:2 * e].reshape(2 * e // P, P).T),
        "b_v": np.ascontiguousarray(bqkv[2 * e:].reshape(1, e)),
        "w_proj": np.ascontiguousarray(L0_gnn_Wproj),
        "b_proj": np.ascontiguousarray(np.asarray(L0_gnn_bproj).reshape(1, e)),
    }
    nc = bacc.Bacc("TRN2", target_bir_lowering=False, num_devices=1)
    args = [nc.dram_tensor(f"in_{name}", a.shape, mybir.dt.from_np(a.dtype), kind="ExternalInput").ap()
            for name, a in arrays.items()]
    out = nc.dram_tensor("out_0", arrays["x"].shape, F32, kind="ExternalOutput").ap()
    graph_attention_block(nc, *args, out)
    r = run_bass_kernel_spmd(nc, [{f"in_{name}": a for name, a in arrays.items()}], core_ids=[0])
    return r.results[0]["out_0"]
```

```python
from contextlib import ExitStack

import concourse.bass as bass
from concourse import mybir

F32 = mybir.dt.float32
F32R = mybir.dt.float32r
I32 = mybir.dt.int32
ALU = mybir.AluOpType
ACT = mybir.ActivationFunctionType
AX_X = mybir.AxisListType.X

P = 128
HEADS = 16
EPS = 1e-5
MASKED = -(2.0 ** 126)
GROUP = 4
QUADRANT = 32
UNROLL = 2


def wait(engine, semaphore, value):
    if isinstance(value, int) and value <= 0:
        return
    engine.wait_ge(semaphore, value)


def graph_attention_block(nc, x, adj, w_qkv, b_qk_columns, b_v, w_proj, b_proj, out):
    BATCHES, N, E = x.shape
    GROUPS = BATCHES // GROUP
    CHUNKS = E // P
    HPC = HEADS // CHUNKS
    DH = E // HEADS
    SCALE = float(DH) ** -0.5
    assert N == P and DH == QUADRANT and CHUNKS == GROUP and GROUPS % UNROLL == 0

    with ExitStack() as ctx:
        def sb(name, shape, dt=F32):
            return ctx.enter_context(nc.sbuf_tensor(name, shape, dt))

        def bank(name):
            return ctx.enter_context(nc.psum_tensor(name, [P, 512], F32))

        def sem(name):
            return ctx.enter_context(nc.semaphore(name))

        wqkv_hi = sb("wqkv_hi", [P, CHUNKS, 3 * E], F32R)
        wqkv_lo = sb("wqkv_lo", [P, CHUNKS, 3 * E], F32R)
        wproj_hi = sb("wproj_hi", [P, CHUNKS, E], F32R)
        wproj_lo = sb("wproj_lo", [P, CHUNKS, E], F32R)
        bqk = sb("bqk", [P, 2 * CHUNKS])
        bv_rows = sb("bv_rows", [P, E])
        bproj_rows = sb("bproj_rows", [P, E])
        identity = sb("identity", [P, P])
        mask_bias = sb("mask_bias", [P, P])
        minus_half = sb("minus_half", [P, 1])
        x_in = sb("x_in", [P, 2, E])
        stats = sb("stats", [P, 6])
        mean_var = sb("mean_var", [P, 2, 2])
        var_eps = sb("var_eps", [P, 2, 1])
        rstd = sb("rstd", [P, 2, 1])
        normed = sb("normed", [P, E])
        ht_hi = sb("ht_hi", [P, 2, CHUNKS, GROUP * N], F32R)
        ht_lo = sb("ht_lo", [P, 2, CHUNKS, GROUP * N], F32R)
        qt_hi = sb("qt_hi", [P, 2, CHUNKS, GROUP * N], F32R)
        qt_lo = sb("qt_lo", [P, 2, CHUNKS, GROUP * N], F32R)
        kt = sb("kt", [P, 2, CHUNKS, GROUP * N])
        v = sb("v", [P, 2 * GROUP, E])
        kdiag_hi = sb("kdiag_hi", [P, CHUNKS, HPC * N], F32R)
        kdiag_lo = sb("kdiag_lo", [P, CHUNKS, HPC * N], F32R)
        probs = sb("probs", [P, CHUNKS, HPC * N])
        row_max = sb("row_max", [P, HEADS])
        neg_max = sb("neg_max", [P, HEADS])
        row_sum = sb("row_sum", [P, HEADS])
        inv_sum = sb("inv_sum", [P, HEADS])
        pt = sb("pt", [P, 2, HPC * N])
        yt_hi = sb("yt_hi", [P, CHUNKS, N], F32R)
        yt_lo = sb("yt_lo", [P, CHUNKS, N], F32R)
        residual = sb("residual", [P, 2, E])

        ps_scores = [bank("ps_scores0"), bank("ps_scores1")]
        ps_pt = [bank("ps_pt0"), bank("ps_pt1")]
        ps_qk = bank("ps_qk")
        ps_vo = bank("ps_vo")
        ps_ht = bank("ps_ht")
        ps_yt = bank("ps_yt")

        def q_bank(attention):
            return ps_qk if attention else ps_scores[0]

        x_loaded = [sem("x_loaded0"), sem("x_loaded1")]
        early_x_loaded = [sem("early_x_loaded0"), sem("early_x_loaded1")]
        res_loaded = [sem("res_loaded0"), sem("res_loaded1")]
        stored = [sem("stored0"), sem("stored1")]
        consts_loaded = sem("consts_loaded")
        w_loaded = [sem("w_k_loaded"), sem("w_q_loaded"), sem("w_v_loaded"), sem("w_proj_loaded")]
        zeroed = sem("zeroed")
        identity_ready = sem("identity_ready")
        mask_step = sem("mask_step")
        w_hi_ready = sem("w_hi_ready")
        w_ready = sem("w_ready")
        stats_ready = sem("stats_ready")
        moments_ready = sem("moments_ready")
        eps_added = sem("eps_added")
        rstd_ready = sem("rstd_ready")
        normed_ready = sem("normed_ready")
        ht_in_psum = sem("ht_in_psum")
        ht_hi_ready = sem("ht_hi_ready")
        ht_ready = sem("ht_ready")
        k_in_psum = sem("k_in_psum")
        kt_ready = sem("kt_ready")
        q_in_psum = sem("q_in_psum")
        q_hi_ready = sem("q_hi_ready")
        q_ready = sem("q_ready")
        v_in_psum = sem("v_in_psum")
        v_ready = sem("v_ready")
        kdiag_hi_ready = sem("kdiag_hi_ready")
        kdiag_ready = sem("kdiag_ready")
        scores_in_psum = sem("scores_in_psum")
        scores_masked = sem("scores_masked")
        max_ready = sem("max_ready")
        neg_max_ready = sem("neg_max_ready")
        exp_ready = sem("exp_ready")
        inv_sum_ready = sem("inv_sum_ready")
        probs_ready = sem("probs_ready")
        pt_in_psum = sem("pt_in_psum")
        pt_ready = sem("pt_ready")
        pv_done = sem("pv_done")
        yt_hi_ready = sem("yt_hi_ready")
        yt_ready = sem("yt_ready")
        proj_in_psum = sem("proj_in_psum")
        res_biased = sem("res_biased")
        out_ready = sem("out_ready")

        def part(w, n):
            return w[:, :, n * E:(n + 1) * E]

        weights = [
            (v[:, 0:GROUP, :], part(wqkv_hi, 1), part(wqkv_lo, 1)),
            (v[:, GROUP:2 * GROUP, :], part(wqkv_hi, 0), part(wqkv_lo, 0)),
            (kt[:, 1, :, :], part(wqkv_hi, 2), part(wqkv_lo, 2)),
            (probs[:, :, :], wproj_hi[:, :, :], wproj_lo[:, :, :]),
        ]
        W_K, W_Q, W_V, W_PROJ = range(4)
        adj_int = pt[:, 0, 0:P].bitcast(I32)

        def x_arrival(i, t):
            slot = t % 2
            if isinstance(i, int) and i == 0:
                return (x_in[:, slot, :], x_loaded[slot], 16) if t < 2 else (residual[:, slot, :], early_x_loaded[slot], 16)
            return x_in[:, slot, :], x_loaded[slot], 16 * (2 * i + t // 2)

        def by_head(tile):
            return tile.rearrange("p (h n) -> p h n", h=HPC)

        def pipeline(engine, step):
            first, last = 3, GROUPS - 1
            turns = (last - first + 1) // UNROLL
            for i in range(first):
                for t in range(GROUP):
                    step(i, t, i % 2, i < GROUPS, 1 <= i, 2 <= i, i == 2 and t == 0)
            with engine.Fori(first, first + turns * UNROLL, UNROLL) as base:
                for u in range(UNROLL):
                    for t in range(GROUP):
                        step(base + u, t, (first + u) % 2, True, True, True, False)
            for i in range(first + turns * UNROLL, GROUPS + 2):
                for t in range(GROUP):
                    step(i, t, i % 2, i < GROUPS, i <= GROUPS, True, False)

        def has_next(i, t):
            return not isinstance(i, int) or 0 <= 4 * (i - 2) + t + 1 < BATCHES

        block = ctx.enter_context(nc.Block())

        @block.sync
        def _(sp):
            def load_x(i, t):
                f = 4 * i + t
                tile, loaded, _ = x_arrival(i, t)
                wait(sp, normed_ready, f - 1 if not (isinstance(i, int) and i == 0) else 0)
                sp.dma_start(tile, x[bass.ds(f, 1)].rearrange("b n e -> (b n) e")).then_inc(loaded, 16)

            def store(b, slot):
                sp.wait_ge(out_ready, b + 1)
                sp.dma_start(out[bass.ds(b, 1)].rearrange("b n e -> (b n) e"), residual[:, slot, :]).then_inc(stored[slot], 16)

            def load_weights(n):
                source = w_proj if n == W_PROJ else w_qkv[:, (E, 0, 2 * E)[n]:(2 * E, E, 3 * E)[n]]
                sp.dma_start(weights[n][0], source.rearrange("(k p) n -> p k n", p=P)).then_inc(w_loaded[n], 16)

            for t in range(GROUP):
                load_x(0, t)
            load_weights(W_K)
            load_weights(W_Q)
            sp.dma_start(adj_int, adj).then_inc(consts_loaded, 16)
            sp.dma_start(bqk[:, :], b_qk_columns).then_inc(consts_loaded, 16)
            sp.dma_start(bv_rows[:, :], b_v.to_broadcast([P, E])).then_inc(consts_loaded, 16)
            sp.dma_start(bproj_rows[:, :], b_proj.to_broadcast([P, E])).then_inc(consts_loaded, 16)
            load_weights(W_V)
            load_weights(W_PROJ)

            def step(i, t, par, front, middle, attention, opening):
                slot = t % 2
                if front and not (isinstance(i, int) and i == 0):
                    load_x(i, t)
                if attention:
                    a = 4 * (i - 2) + t
                    earlier = isinstance(i, int) and i == 2 and t < 2
                    if not earlier:
                        store(a - 2, slot)
                        sp.wait_ge(stored[slot], 16 * (2 * (i - 2) + t // 2))
                    sp.dma_start(residual[:, slot, :], x[bass.ds(a, 1)].rearrange("b n e -> (b n) e")).then_inc(res_loaded[slot], 16)

            pipeline(sp, step)
            for b in (BATCHES - 2, BATCHES - 1):
                store(b, b % 2)
            for slot in range(2):
                sp.wait_ge(stored[slot], 16 * (BATCHES // 2))

        @block.gpsimd
        def _(pool):
            nc.gpsimd.memset(identity[:, :], 0.0).then_inc(zeroed, 1)
            nc.gpsimd.memset(minus_half[:, :], -0.5).then_inc(zeroed, 1)
            pool.wait_ge(zeroed, 2)
            nc.gpsimd.affine_select(out=identity[:, :], in_=identity[:, :], compare_op=ALU.not_equal, fill=1.0, base=0,
                                    pattern=[[-1, P]], channel_multiplier=1).then_inc(identity_ready, 1)
            nc.gpsimd.memset(kdiag_hi[:, :, :].bitcast(F32), 0.0).then_inc(zeroed, 1)
            nc.gpsimd.memset(kdiag_lo[:, :, :].bitcast(F32), 0.0).then_inc(zeroed, 1)

            def inverse_std(f, slot):
                pool.wait_ge(eps_added, f + 1)
                nc.gpsimd.tensor_tensor(rstd[:, slot, :], var_eps[:, slot, :], minus_half[:, :], ALU.pow).then_inc(rstd_ready, 1)

            def normalise_probs(a, c):
                pool.wait_ge(inv_sum_ready, 4 * a + c + 1)
                heads = slice(HPC * c, HPC * (c + 1))
                nc.gpsimd.tensor_tensor(by_head(probs[:, c, :]), by_head(probs[:, c, :]),
                                        inv_sum[:, heads].unsqueeze(2).to_broadcast([P, HPC, N]),
                                        ALU.mult).then_inc(probs_ready, 1)

            def step(i, t, par, front, middle, attention, opening):
                a = 4 * (i - 2) + t
                if attention:
                    slot = t % 2
                    pool.wait_ge(res_loaded[slot], 16 * (2 * (i - 2) + t // 2 + 1))
                    pool.wait_ge(consts_loaded, 64)
                    nc.gpsimd.tensor_tensor(residual[:, slot, :], residual[:, slot, :], bproj_rows[:, :],
                                            ALU.add).then_inc(res_biased, 1)
                    normalise_probs(a, 0)
                if front:
                    inverse_std(4 * i + t, t % 2)
                if attention:
                    normalise_probs(a, 1)
                    normalise_probs(a, 2)
                    normalise_probs(a, 3)

            pipeline(pool, step)

        @block.scalar
        def _(act):
            def split_high(n):
                act.wait_ge(w_loaded[n], 16)
                stage, high, _ = weights[n]
                nc.scalar.activation(high, stage, ACT.Copy).then_inc(w_hi_ready, 1)

            def exp_chunk(a, c):
                act.wait_ge(neg_max_ready, 4 * a + c + 1)
                for h in range(HPC * c, HPC * (c + 1)):
                    tile = probs[:, c, N * (h % HPC):N * (h % HPC + 1)]
                    last = nc.scalar.activation(tile, tile, ACT.Exp, bias=neg_max[:, h:h + 1], accum_out=row_sum[:, h:h + 1])
                last.then_inc(exp_ready, 1)

            def pt_chunk(a, c):
                act.wait_ge(pt_in_psum, 4 * a + c + 1)
                wait(act, pv_done, 4 * a + c - 1)
                nc.scalar.activation(pt[:, c % 2, :], ps_pt[c % 2][:, :], ACT.Copy).then_inc(pt_ready, 1)

            def step(i, t, par, front, middle, attention, opening):
                f, m, a = 4 * i + t, 4 * (i - 1) + t, 4 * (i - 2) + t
                if attention:
                    exp_chunk(a, 0)
                if middle:
                    if isinstance(i, int) and i == 1 and t == 0:
                        act.wait_ge(consts_loaded, 64)
                    act.wait_ge(k_in_psum, m + 1)
                    wait(act, kdiag_ready, 16 * (i - 2))
                    nc.scalar.activation(kt[:, 1 - par, t, :], ps_qk[:, :], ACT.Identity,
                                         bias=bqk[:, CHUNKS + t:CHUNKS + t + 1]).then_inc(kt_ready, 1)
                if attention:
                    exp_chunk(a, 1)
                    exp_chunk(a, 2)
                    exp_chunk(a, 3)
                    pt_chunk(a, 0)
                if middle:
                    act.wait_ge(q_in_psum, m + 1)
                    wait(act, scores_in_psum, 16 * (i - 2))
                    nc.scalar.activation(qt_hi[:, 1 - par, t, :], q_bank(attention)[:, :], ACT.Identity,
                                         bias=bqk[:, t:t + 1]).then_inc(q_hi_ready, 1)
                if attention:
                    pt_chunk(a, 1)
                    pt_chunk(a, 2)
                    pt_chunk(a, 3)
                if front:
                    act.wait_ge(ht_in_psum, f + 1)
                    wait(act, v_in_psum, 4 * (i - 1))
                    nc.scalar.activation(ht_hi[:, par, :, N * t:N * (t + 1)], ps_ht[:, :].rearrange("p (k n) -> p k n", k=CHUNKS),
                                         ACT.Relu).then_inc(ht_hi_ready, 1)
                if attention:
                    act.wait_ge(pv_done, 4 * (a + 1))
                    wait(act, proj_in_psum, a)
                    nc.scalar.activation(yt_hi[:, :, :], ps_yt[:, :].rearrange("p (c n) -> p c n", c=CHUNKS),
                                         ACT.Copy).then_inc(yt_hi_ready, 1)
                if isinstance(i, int) and (i, t) in ((0, 0), (0, 1), (0, 3), (1, 0)):
                    split_high({(0, 0): W_K, (0, 1): W_Q, (0, 3): W_V, (1, 0): W_PROJ}[i, t])

            pipeline(act, step)

        @block.vector
        def _(dve):
            def row_stats(i, t):
                tile, loaded, count = x_arrival(i, t)
                dve.wait_ge(loaded, count)
                nc.vector.bn_stats(stats[:, :], tile).then_inc(stats_ready, 1)

            def moments(f, slot):
                nc.vector.bn_aggr(mean_var[:, slot, :], stats[:, :]).then_inc(moments_ready, 1)
                dve.wait_ge(moments_ready, f + 1)
                nc.vector.tensor_scalar(var_eps[:, slot, :], mean_var[:, slot, 1:2], EPS, None, ALU.add).then_inc(eps_added, 1)

            def normalise(i, t):
                f, slot = 4 * i + t, t % 2
                dve.wait_ge(rstd_ready, f + 1)
                wait(dve, ht_in_psum, f)
                nc.vector.tensor_scalar(normed[:, :], x_arrival(i, t)[0], mean_var[:, slot, 0:1], rstd[:, slot, :],
                                        ALU.subtract, ALU.mult).then_inc(normed_ready, 1)

            def split_low(n):
                dve.wait_ge(w_hi_ready, n + 1)
                stage, high, low = weights[n]
                nc.vector.tensor_tensor(low, stage, high.bitcast(F32), ALU.subtract).then_inc(w_ready, 1)

            def keep_v(m, i, t, par):
                dve.wait_ge(v_in_psum, m + 1)
                wait(dve, pv_done, 16 * (i - 2))
                nc.vector.tensor_tensor(v[:, GROUP * (1 - par) + t, :], ps_vo[:, :], bv_rows[:, :], ALU.add).then_inc(v_ready, 1)

            def low_ht(f, t, par):
                dve.wait_ge(ht_hi_ready, f + 1)
                nc.vector.scalar_tensor_tensor(out=ht_lo[:, par, :, N * t:N * (t + 1)],
                                               in0=ps_ht[:, :].rearrange("p (k n) -> p k n", k=CHUNKS), scalar=0.0,
                                               in1=ht_hi[:, par, :, N * t:N * (t + 1)].bitcast(F32),
                                               op0=ALU.max, op1=ALU.subtract).then_inc(ht_ready, 1)

            def make_mask():
                dve.wait_ge(consts_loaded, 64)
                dve.wait_ge(identity_ready, 1)
                nc.vector.tensor_tensor(mask_bias[:, :], adj_int, identity[:, :], ALU.add).then_inc(mask_step, 1)
                dve.wait_ge(mask_step, 1)
                nc.vector.tensor_scalar(mask_bias[:, :], mask_bias[:, :], 0.0, None, ALU.is_gt).then_inc(mask_step, 1)
                dve.wait_ge(mask_step, 2)
                nc.vector.tensor_scalar(mask_bias[:, :], mask_bias[:, :], 1.0, -MASKED, ALU.subtract, ALU.mult).then_inc(mask_step, 1)
                dve.wait_ge(mask_step, 3)

            def masked_max(a, c):
                dve.wait_ge(scores_in_psum, 4 * a + c + 1)
                wait(dve, pt_in_psum, 4 * a + c - 3)
                nc.vector.scalar_tensor_tensor(out=by_head(probs[:, c, :]), in0=by_head(ps_scores[c % 2][:, :]), scalar=SCALE,
                                               in1=mask_bias[:, :].unsqueeze(1).to_broadcast([P, HPC, N]),
                                               op0=ALU.mult, op1=ALU.add).then_inc(scores_masked, 1)
                heads = slice(HPC * c, HPC * (c + 1))
                dve.wait_ge(scores_masked, 4 * a + c + 1)
                nc.vector.tensor_reduce(row_max[:, heads], by_head(probs[:, c, :]), AX_X, ALU.max).then_inc(max_ready, 1)
                dve.wait_ge(max_ready, 4 * a + c + 1)
                nc.vector.tensor_scalar(neg_max[:, heads], row_max[:, heads], -1.0, None, ALU.mult).then_inc(neg_max_ready, 1)

            def invert_sum(a, c):
                heads = slice(HPC * c, HPC * (c + 1))
                dve.wait_ge(exp_ready, 4 * a + c + 1)
                nc.vector.reciprocal(inv_sum[:, heads], row_sum[:, heads]).then_inc(inv_sum_ready, 1)

            def step(i, t, par, front, middle, attention, opening):
                f, m, a = 4 * i + t, 4 * (i - 1) + t, 4 * (i - 2) + t
                if isinstance(i, int) and (i, t) == (1, 0):
                    split_low(W_V)
                if isinstance(i, int) and (i, t) == (1, 1):
                    split_low(W_PROJ)
                    make_mask()
                if attention:
                    masked_max(a, 0)
                if front:
                    row_stats(i, t)
                if attention:
                    masked_max(a, 1)
                if front:
                    dve.wait_ge(stats_ready, f + 1)
                if attention:
                    invert_sum(a, 0)
                if front:
                    moments(f, t % 2)
                    if not middle and t > 0:
                        low_ht(f - 1, t - 1, par)
                        if t == 2:
                            split_low(W_K)
                if attention:
                    masked_max(a, 2)
                    invert_sum(a, 1)
                    masked_max(a, 3)
                    invert_sum(a, 2)
                if has_next(i, t):
                    nxt, npar, nt = (a + 1, par if t < 3 else 1 - par, (t + 1) % GROUP)
                    dve.wait_ge(kt_ready, group_steps(i, t))
                    if attention:
                        dve.wait_ge(scores_in_psum, 4 * (a + 1))
                    dve.wait_ge(zeroed, 4)
                    for j in range(HPC):
                        rows = slice(QUADRANT * j, QUADRANT * (j + 1))
                        nc.vector.tensor_copy(kdiag_hi[rows, :, N * j:N * (j + 1)],
                                              kt[rows, npar, :, N * nt:N * (nt + 1)]).then_inc(kdiag_hi_ready, 1)
                if attention and not opening:
                    add_residual(a - 1, (t - 1) % 2)
                if attention:
                    invert_sum(a, 3)
                if has_next(i, t):
                    for j in range(HPC):
                        rows = slice(QUADRANT * j, QUADRANT * (j + 1))
                        dve.wait_ge(kdiag_hi_ready, 4 * nxt + j + 1)
                        nc.vector.tensor_tensor(kdiag_lo[rows, :, N * j:N * (j + 1)], kt[rows, npar, :, N * nt:N * (nt + 1)],
                                                kdiag_hi[rows, :, N * j:N * (j + 1)].bitcast(F32),
                                                ALU.subtract).then_inc(kdiag_ready, 1)
                if front:
                    normalise(i, t)
                if middle and not attention:
                    keep_v(m, i, t, par)
                if middle:
                    dve.wait_ge(q_hi_ready, m + 1)
                    nc.vector.scalar_tensor_tensor(out=qt_lo[:, 1 - par, t, :], in0=q_bank(attention)[:, :], scalar=bqk[:, t:t + 1],
                                                   in1=qt_hi[:, 1 - par, t, :].bitcast(F32),
                                                   op0=ALU.add, op1=ALU.subtract).then_inc(q_ready, 1)
                if middle and attention:
                    keep_v(m, i, t, par)
                if front and middle:
                    low_ht(f, t, par)
                if front and not middle and t == GROUP - 1:
                    low_ht(f, t, par)
                    split_low(W_Q)
                if attention:
                    dve.wait_ge(yt_hi_ready, a + 1)
                    nc.vector.tensor_tensor(yt_lo[:, :, :], ps_yt[:, :].rearrange("p (c n) -> p c n", c=CHUNKS),
                                            yt_hi[:, :, :].bitcast(F32), ALU.subtract).then_inc(yt_ready, 1)

            def group_steps(i, t):
                return 4 * (i - 1) if t < GROUP - 1 else 4 * i

            def add_residual(b, slot):
                dve.wait_ge(proj_in_psum, b + 1)
                dve.wait_ge(res_biased, b + 1)
                nc.vector.tensor_tensor(residual[:, slot, :], ps_vo[:, :], residual[:, slot, :], ALU.add).then_inc(out_ready, 1)

            pipeline(dve, step)
            add_residual(BATCHES - 1, (BATCHES - 1) % 2)

        @block.tensor
        def _(pe):
            pe.wait_ge(identity_ready, 1)

            def three_passes(out_tile, stationary, moving, ks, first, last):
                (s_hi, s_lo), (m_hi, m_lo) = stationary, moving
                for k in ks:
                    for n, (s, m) in enumerate(((s_hi, m_hi), (s_hi, m_lo), (s_lo, m_hi))):
                        done = nc.tensor.matmul(out_tile, s(k), m(k), start=(first and k == ks[0] and n == 0),
                                                stop=(last and k == ks[-1] and n == 2))
                return done

            def projection(out_tile, stationary, moving, half):
                ks = list(range(CHUNKS // 2)) if half == 0 else list(range(CHUNKS // 2, CHUNKS))
                return three_passes(out_tile, stationary, moving, ks, half == 0, half == 1)

            def parts(hi, lo, at):
                return (lambda k: at(hi, k)), (lambda k: at(lo, k))

            def qk_half(bank, i, t, par, offset, half):
                return projection(bank[:, :],
                                  parts(wqkv_hi, wqkv_lo, lambda w, k: w[:, k, offset + P * t:offset + P * (t + 1)]),
                                  parts(ht_hi, ht_lo, lambda h, k: h[:, 1 - par, k, :]), half)

            def k_half(i, t, par, half, attention, opening):
                m = 4 * (i - 1) + t
                if half == 0:
                    if t == 0:
                        pe.wait_ge(w_ready, W_K + 1)
                        pe.wait_ge(ht_ready, 4 * i)
                    if attention and not opening:
                        pe.wait_ge(q_ready, m)
                    else:
                        wait(pe, kt_ready, m)
                done = qk_half(ps_qk, i, t, par, E, half)
                if half == 1:
                    done.then_inc(k_in_psum, 1)

            def q_half(i, t, par, half, attention):
                m = 4 * (i - 1) + t
                if half == 0:
                    if t == 0:
                        pe.wait_ge(w_ready, W_Q + 1)
                    if attention:
                        pe.wait_ge(kt_ready, m + 1)
                    else:
                        wait(pe, q_ready, m)
                done = qk_half(q_bank(attention), i, t, par, 0, half)
                if half == 1:
                    done.then_inc(q_in_psum, 1)

            def v_half(i, t, par, half, after_projection):
                if half == 0 and t == 0:
                    pe.wait_ge(w_ready, W_V + 1)
                if half == 0 and after_projection:
                    pe.wait_ge(out_ready, 4 * (i - 2) + t)
                elif half == 0:
                    wait(pe, v_ready, 4 * (i - 1) + t)
                done = projection(ps_vo[:, :],
                                  parts(ht_hi, ht_lo, lambda h, k: h[:, 1 - par, k, N * t:N * (t + 1)]),
                                  parts(wqkv_hi, wqkv_lo, lambda w, k: w[:, k, 2 * E:3 * E]), half)
                if half == 1:
                    done.then_inc(v_in_psum, 1)

            def proj_half(b, vs, half):
                if half == 0:
                    pe.wait_ge(w_ready, W_PROJ + 1)
                    pe.wait_ge(yt_ready, b + 1)
                    pe.wait_ge(v_ready, vs)
                done = projection(ps_vo[:, :], parts(yt_hi, yt_lo, lambda y, k: y[:, k, :]),
                                  parts(wproj_hi, wproj_lo, lambda w, k: w[:, k, :]), half)
                if half == 1:
                    done.then_inc(proj_in_psum, 1)

            def scores(i, t, par, c):
                a = 4 * (i - 2) + t
                if c == 0:
                    pe.wait_ge(kdiag_ready, 4 * (a + 1))
                    if t == 0:
                        pe.wait_ge(q_ready, 4 * (i - 1))
                wait(pe, scores_masked, 4 * a + c - 1)
                three_passes(ps_scores[c % 2][:, :],
                             parts(qt_hi, qt_lo, lambda q, _: q[:, par, c, N * t:N * (t + 1)]),
                             parts(kdiag_hi, kdiag_lo, lambda k, _: k[:, c, :]), [0], True, True).then_inc(scores_in_psum, 1)

            def transpose_probs(a, c):
                pe.wait_ge(probs_ready, 4 * a + c + 1)
                wait(pe, pt_ready, 4 * a + c - 1)
                for j in range(HPC):
                    last = nc.tensor.transpose(ps_pt[c % 2][:, N * j:N * (j + 1)], probs[:, c, N * j:N * (j + 1)], identity[:, :])
                last.then_inc(pt_in_psum, 1)

            def pv(i, t, par, c):
                a = 4 * (i - 2) + t
                if c == 0:
                    pe.wait_ge(v_ready, a + 1)
                    wait(pe, yt_ready, a)
                pe.wait_ge(pt_ready, 4 * a + c + 1)
                for j in range(HPC):
                    h = HPC * c + j
                    last = nc.tensor.matmul(ps_yt[QUADRANT * j:QUADRANT * (j + 1), N * c:N * (c + 1)],
                                            v[:, GROUP * par + t, DH * h:DH * (h + 1)],
                                            pt[:, c % 2, N * j:N * (j + 1)], start=True, stop=True)
                last.then_inc(pv_done, 1)

            def transpose_rows(f):
                pe.wait_ge(normed_ready, f + 1)
                wait(pe, ht_ready, f)
                for k in range(CHUNKS):
                    last = nc.tensor.transpose(ps_ht[:, N * k:N * (k + 1)], normed[:, P * k:P * (k + 1)], identity[:, :])
                last.then_inc(ht_in_psum, 1)

            def step(i, t, par, front, middle, attention, opening):
                f, a = 4 * i + t, 4 * (i - 2) + t
                v_steps = 4 * (i - 1) + t
                if not middle or (isinstance(i, int) and i > GROUPS):
                    v_steps = BATCHES
                if attention:
                    scores(i, t, par, 0)
                if middle:
                    k_half(i, t, par, 0, attention, opening)
                if attention:
                    scores(i, t, par, 1)
                if middle:
                    k_half(i, t, par, 1, attention, opening)
                if attention:
                    scores(i, t, par, 2)
                    if not opening:
                        proj_half(a - 1, v_steps, 0)
                    scores(i, t, par, 3)
                    if not opening:
                        proj_half(a - 1, v_steps, 1)
                if middle and not attention:
                    v_half(i, t, par, 0, False)
                    v_half(i, t, par, 1, False)
                if middle:
                    q_half(i, t, par, 0, attention)
                if attention:
                    transpose_probs(a, 0)
                if middle:
                    q_half(i, t, par, 1, attention)
                if attention:
                    transpose_probs(a, 1)
                if middle and attention:
                    v_half(i, t, par, 0, not opening)
                if attention:
                    transpose_probs(a, 2)
                    pv(i, t, par, 0)
                if middle and attention:
                    v_half(i, t, par, 1, not opening)
                if attention:
                    transpose_probs(a, 3)
                    pv(i, t, par, 1)
                if front:
                    transpose_rows(f)
                if attention:
                    pv(i, t, par, 2)
                    pv(i, t, par, 3)

            pipeline(pe, step)
            proj_half(BATCHES - 1, BATCHES, 0)
            proj_half(BATCHES - 1, BATCHES, 1)


def kernel(x, adj, L0_gnn_Wqkv, L0_gnn_bqkv, L0_gnn_Wproj, L0_gnn_bproj):
    import numpy as np
    import concourse.bacc as bacc
    from concourse.bass_utils import run_bass_kernel_spmd

    e = L0_gnn_Wproj.shape[0]
    bqkv = np.asarray(L0_gnn_bqkv)
    arrays = {
        "x": np.ascontiguousarray(x),
        "adj": np.ascontiguousarray(adj),
        "w_qkv": np.ascontiguousarray(L0_gnn_Wqkv),
        "b_qk_columns": np.ascontiguousarray(bqkv[:2 * e].reshape(2 * e // P, P).T),
        "b_v": np.ascontiguousarray(bqkv[2 * e:].reshape(1, e)),
        "w_proj": np.ascontiguousarray(L0_gnn_Wproj),
        "b_proj": np.ascontiguousarray(np.asarray(L0_gnn_bproj).reshape(1, e)),
    }
    nc = bacc.Bacc("TRN2", target_bir_lowering=False, num_devices=1)
    args = [nc.dram_tensor(f"in_{name}", a.shape, mybir.dt.from_np(a.dtype), kind="ExternalInput").ap()
            for name, a in arrays.items()]
    out = nc.dram_tensor("out_0", arrays["x"].shape, F32, kind="ExternalOutput").ap()
    graph_attention_block(nc, *args, out)
    r = run_bass_kernel_spmd(nc, [{f"in_{name}": a for name, a in arrays.items()}], core_ids=[0])
    return r.results[0]["out_0"]
```

```python
from contextlib import ExitStack

import concourse.bass as bass
from concourse import mybir

F32 = mybir.dt.float32
F32R = mybir.dt.float32r
I32 = mybir.dt.int32
ALU = mybir.AluOpType
ACT = mybir.ActivationFunctionType
AX_X = mybir.AxisListType.X

P = 128
HEADS = 16
EPS = 1e-5
MASKED = 2.0 ** 126
GROUP = 4
QUADRANT = 32
UNROLL = 2


def wait(engine, semaphore, value):
    if isinstance(value, int) and value <= 0:
        return
    engine.wait_ge(semaphore, value)


def graph_attention_block(nc, x, adj, w_qkv, b_qk_columns, b_v_columns, w_proj, b_proj, out):
    BATCHES, N, E = x.shape
    GROUPS = BATCHES // GROUP
    CHUNKS = E // P
    HPC = HEADS // CHUNKS
    DH = E // HEADS
    SCALE = float(DH) ** -0.5
    assert N == P and DH == QUADRANT and CHUNKS == GROUP and GROUPS % UNROLL == 0

    with ExitStack() as ctx:
        def sb(name, shape, dt=F32):
            return ctx.enter_context(nc.sbuf_tensor(name, shape, dt))

        def bank(name):
            return ctx.enter_context(nc.psum_tensor(name, [P, 512], F32))

        def sem(name):
            return ctx.enter_context(nc.semaphore(name))

        wqkv_hi = sb("wqkv_hi", [P, CHUNKS, 3 * E], F32R)
        wqkv_lo = sb("wqkv_lo", [P, CHUNKS, 3 * E], F32R)
        wproj_hi = sb("wproj_hi", [P, CHUNKS, E], F32R)
        wproj_lo = sb("wproj_lo", [P, CHUNKS, E], F32R)
        bqk = sb("bqk", [P, 2 * CHUNKS])
        bv = sb("bv", [P, CHUNKS])
        out_bias = sb("out_bias", [P, E])
        identity = sb("identity", [P, P])
        mask_bias = sb("mask_bias", [P, P])
        minus_half = sb("minus_half", [P, 1])
        x_in = sb("x_in", [P, 2, E])
        stats = sb("stats", [P, 6])
        mean_var = sb("mean_var", [P, 2, 2])
        var_eps = sb("var_eps", [P, 2, 1])
        rstd = sb("rstd", [P, 2, 1])
        ht_hi = sb("ht_hi", [P, 2, CHUNKS, GROUP * N], F32R)
        ht_lo = sb("ht_lo", [P, 2, CHUNKS, GROUP * N], F32R)
        q_pairs = sb("q_pairs", [P, 2, CHUNKS, 2, GROUP * N], F32R)
        kt = sb("kt", [P, 2, CHUNKS, GROUP * N])
        v = sb("v", [P, 2 * GROUP, E])
        kdiag_hi = sb("kdiag_hi", [P, CHUNKS, 2, 2, N], F32R)
        kdiag_lo = sb("kdiag_lo", [P, CHUNKS, 2, 2, N], F32R)
        probs = sb("probs", [P, CHUNKS, HPC * N])
        neg_max = sb("neg_max", [P, HEADS])
        row_sum = sb("row_sum", [P, HEADS])
        inv_sum = sb("inv_sum", [P, HEADS])
        pt = sb("pt", [P, CHUNKS, HPC * N])
        yt_hi = sb("yt_hi", [P, CHUNKS, N], F32R)
        yt_lo = sb("yt_lo", [P, CHUNKS, N], F32R)
        residual = sb("residual", [P, 2, E])

        ps_scores = [bank("ps_scores0"), bank("ps_scores1")]
        ps_pt = [bank("ps_pt0"), bank("ps_pt1")]
        ps_qk = bank("ps_qk")
        ps_vo = bank("ps_vo")
        ps_ht = bank("ps_ht")
        ps_yt = bank("ps_yt")

        def q_bank(attention):
            return ps_qk if attention else ps_scores[0]

        def ht_bank(i, t):
            return (ps_ht, ps_yt, ps_vo, ps_pt[0])[t] if isinstance(i, int) and i == 0 else ps_ht

        x_loaded = [sem("x_loaded0"), sem("x_loaded1")]
        early_x_loaded = [sem("early_x_loaded0"), sem("early_x_loaded1")]
        res_loaded = [sem("res_loaded0"), sem("res_loaded1")]
        stored = [sem("stored0"), sem("stored1")]
        consts_loaded = sem("consts_loaded")
        w_loaded = [sem("w_k_loaded"), sem("w_q_loaded"), sem("w_v_loaded"), sem("w_proj_loaded")]
        zeroed = sem("zeroed")
        identity_ready = sem("identity_ready")
        mask_step = sem("mask_step")
        w_hi_ready = sem("w_hi_ready")
        w_ready = sem("w_ready")
        bv_wide_ready = sem("bv_wide_ready")
        bv_projected = sem("bv_projected")
        out_bias_ready = sem("out_bias_ready")
        stats_ready = sem("stats_ready")
        moments_ready = sem("moments_ready")
        eps_added = sem("eps_added")
        rstd_ready = sem("rstd_ready")
        normed_ready = sem("normed_ready")
        ht_in_psum = sem("ht_in_psum")
        ht_hi_ready = sem("ht_hi_ready")
        ht_ready = sem("ht_ready")
        k_in_psum = sem("k_in_psum")
        kt_ready = sem("kt_ready")
        q_in_psum = sem("q_in_psum")
        q_hi_ready = sem("q_hi_ready")
        q_ready = sem("q_ready")
        v_in_psum = sem("v_in_psum")
        v_ready = sem("v_ready")
        kdiag_hi_ready = sem("kdiag_hi_ready")
        kdiag_shifted_ready = sem("kdiag_shifted_ready")
        kdiag_ready = sem("kdiag_ready")
        scores_in_psum = sem("scores_in_psum")
        scores_masked = sem("scores_masked")
        neg_max_ready = sem("neg_max_ready")
        exp_ready = sem("exp_ready")
        inv_sum_ready = sem("inv_sum_ready")
        probs_ready = sem("probs_ready")
        pt_in_psum = sem("pt_in_psum")
        pt_ready = sem("pt_ready")
        pv_done = sem("pv_done")
        yt_hi_ready = sem("yt_hi_ready")
        yt_ready = sem("yt_ready")
        proj_in_psum = sem("proj_in_psum")
        res_biased = sem("res_biased")
        out_ready = sem("out_ready")

        def part(w, n):
            return w[:, :, n * E:(n + 1) * E]

        weights = [
            (v[:, 0:GROUP, :], part(wqkv_hi, 1), part(wqkv_lo, 1)),
            (v[:, GROUP:2 * GROUP, :], part(wqkv_hi, 0), part(wqkv_lo, 0)),
            (kt[:, 1, :, :], part(wqkv_hi, 2), part(wqkv_lo, 2)),
            (probs[:, :, :], wproj_hi[:, :, :], wproj_lo[:, :, :]),
        ]
        W_K, W_Q, W_V, W_PROJ = range(4)
        pieces = [(W_K, slice(0, P)), (W_Q, slice(0, P)), (W_V, slice(0, E)),
                  (W_K, slice(P, E)), (W_Q, slice(P, E)), (W_PROJ, slice(0, E))]
        K_FIRST, Q_FIRST, V_ALL, K_REST, Q_REST, PROJ_ALL = range(6)
        adj_int = pt[:, 0, 0:P].bitcast(I32)

        def x_arrival(i, t):
            slot = t % 2
            if isinstance(i, int) and i == 0:
                return (x_in[:, slot, :], x_loaded[slot], 16) if t < 2 else (residual[:, slot, :], early_x_loaded[slot], 16)
            return x_in[:, slot, :], x_loaded[slot], 16 * (2 * i + t // 2)

        HALF = P // 2

        def half_rows(jj):
            return slice(HALF * jj, HALF * (jj + 1))

        def spread(j, shifted):
            quadrant = (j + 2) % 4 if shifted else j
            return slice(QUADRANT * quadrant, QUADRANT * (quadrant + 1)), j // 2, j % 2

        def by_head(tile):
            return tile.rearrange("p (h n) -> p h n", h=HPC)

        def pipeline(engine, step, attention_step):
            first, last = 3, GROUPS - 1
            turns = (last - first + 1) // UNROLL
            for i in range(first):
                for t in range(GROUP):
                    step(i, t, i % 2, i < GROUPS, 1 <= i, 2 <= i, i == 2 and t == 0)
            with engine.Fori(first, first + turns * UNROLL, UNROLL) as base:
                for u in range(UNROLL):
                    for t in range(GROUP):
                        step(base + u, t, (first + u) % 2, True, True, True, False)
            for i in range(first + turns * UNROLL, GROUPS + 1):
                for t in range(GROUP):
                    step(i, t, i % 2, i < GROUPS, True, True, False)
            for t in range(GROUP):
                attention_step(GROUPS + 1, t, (GROUPS + 1) % 2)

        def has_next(i, t):
            return not isinstance(i, int) or 0 <= 4 * (i - 2) + t + 1 < BATCHES

        def next_batch(t, par):
            return (par if t < GROUP - 1 else 1 - par), (t + 1) % GROUP

        def group_steps(i, t):
            return 4 * (i - 1) if t < GROUP - 1 else 4 * i

        block = ctx.enter_context(nc.Block())

        @block.sync
        def _(sp):
            def load_x(i, t):
                f = 4 * i + t
                tile, loaded, _ = x_arrival(i, t)
                if not (isinstance(i, int) and i == 0):
                    sp.wait_ge(ht_in_psum, f - 1)
                sp.dma_start(tile, x[bass.ds(f, 1)].rearrange("b n e -> (b n) e")).then_inc(loaded, 16)

            def store(b, slot):
                sp.wait_ge(out_ready, b + 1)
                sp.dma_start(out[bass.ds(b, 1)].rearrange("b n e -> (b n) e"), residual[:, slot, :]).then_inc(stored[slot], 16)

            def load_weights(n):
                source = w_proj if n == W_PROJ else w_qkv[:, (E, 0, 2 * E)[n]:(2 * E, E, 3 * E)[n]]
                sp.dma_start(weights[n][0], source.rearrange("(k p) n -> p k n", p=P)).then_inc(w_loaded[n], 16)

            for t in range(GROUP):
                load_x(0, t)
            load_weights(W_K)
            load_weights(W_Q)
            sp.dma_start(adj_int, adj).then_inc(consts_loaded, 16)
            sp.dma_start(bqk[:, :], b_qk_columns).then_inc(consts_loaded, 16)
            sp.dma_start(bv[:, :], b_v_columns).then_inc(consts_loaded, 16)
            sp.dma_start(out_bias[:, :], b_proj.to_broadcast([P, E])).then_inc(consts_loaded, 16)
            load_weights(W_V)
            load_weights(W_PROJ)

            def step(i, t, par, front, middle, attention, opening):
                slot = t % 2
                if front and not (isinstance(i, int) and i == 0):
                    load_x(i, t)
                if attention:
                    a = 4 * (i - 2) + t
                    slot_unused = isinstance(i, int) and i == 2 and t < 2
                    if not slot_unused:
                        store(a - 2, slot)
                        sp.wait_ge(stored[slot], 16 * (2 * (i - 2) + t // 2))
                    sp.dma_start(residual[:, slot, :], x[bass.ds(a, 1)].rearrange("b n e -> (b n) e")).then_inc(res_loaded[slot], 16)

            pipeline(sp, step, lambda i, t, par: step(i, t, par, False, False, True, False))
            for b in (BATCHES - 2, BATCHES - 1):
                store(b, b % 2)
            for slot in range(2):
                sp.wait_ge(stored[slot], 16 * (BATCHES // 2))

        @block.gpsimd
        def _(pool):
            nc.gpsimd.memset(identity[:, :], 0.0).then_inc(zeroed, 1)
            nc.gpsimd.memset(minus_half[:, :], -0.5).then_inc(zeroed, 1)
            pool.wait_ge(zeroed, 2)
            nc.gpsimd.affine_select(out=identity[:, :], in_=identity[:, :], compare_op=ALU.not_equal, fill=1.0, base=0,
                                    pattern=[[-1, P]], channel_multiplier=1).then_inc(identity_ready, 1)
            nc.gpsimd.memset(kdiag_hi[:, :, :, :, :].bitcast(F32), 0.0).then_inc(zeroed, 1)
            nc.gpsimd.memset(kdiag_lo[:, :, :, :, :].bitcast(F32), 0.0).then_inc(zeroed, 1)

            def inverse_std(f, slot):
                pool.wait_ge(eps_added, f + 1)
                nc.gpsimd.tensor_tensor(rstd[:, slot, :], var_eps[:, slot, :], minus_half[:, :], ALU.pow).then_inc(rstd_ready, 1)

            def bias_residual(i, t):
                slot = t % 2
                pool.wait_ge(res_loaded[slot], 16 * (2 * (i - 2) + t // 2 + 1))
                pool.wait_ge(out_bias_ready, 1)
                nc.gpsimd.tensor_tensor(residual[:, slot, :], residual[:, slot, :], out_bias[:, :],
                                        ALU.add).then_inc(res_biased, 1)

            def normalise_probs(a, c):
                pool.wait_ge(inv_sum_ready, 4 * a + c + 1)
                heads = slice(HPC * c, HPC * (c + 1))
                nc.gpsimd.tensor_tensor(by_head(probs[:, c, :]), by_head(probs[:, c, :]),
                                        inv_sum[:, heads].unsqueeze(2).to_broadcast([P, HPC, N]),
                                        ALU.mult).then_inc(probs_ready, 1)

            def step(i, t, par, front, middle, attention, opening):
                a = 4 * (i - 2) + t
                if attention:
                    if not opening:
                        bias_residual(i, t)
                    normalise_probs(a, 0)
                if front:
                    inverse_std(4 * i + t, t % 2)
                if attention:
                    normalise_probs(a, 1)
                    normalise_probs(a, 2)
                    normalise_probs(a, 3)
                    if opening:
                        bias_residual(i, t)

            def attention_step(i, t, par):
                a = 4 * (i - 2) + t
                for c in range(CHUNKS):
                    normalise_probs(a, c)
                bias_residual(i, t)

            pipeline(pool, step, attention_step)

        @block.scalar
        def _(act):
            def split_high(piece):
                n, columns = pieces[piece]
                act.wait_ge(w_loaded[n], 16)
                stage, high, _ = weights[n]
                nc.scalar.activation(high[:, :, columns], stage[:, :, columns], ACT.Copy).then_inc(w_hi_ready, 1)

            def exp_chunk(a, c):
                act.wait_ge(neg_max_ready, 4 * a + c + 1)
                for h in range(HPC * c, HPC * (c + 1)):
                    tile = probs[:, c, N * (h % HPC):N * (h % HPC + 1)]
                    last = nc.scalar.activation(tile, tile, ACT.Exp, bias=neg_max[:, h:h + 1], scale=-1.0,
                                                accum_out=row_sum[:, h:h + 1])
                last.then_inc(exp_ready, 1)

            def keep_v(m, i, t, par):
                act.wait_ge(v_in_psum, m + 1)
                wait(act, pv_done, 16 * (i - 2))
                nc.scalar.activation(v[:, GROUP * (1 - par) + t, :], ps_vo[:, :], ACT.Copy).then_inc(v_ready, 1)

            def pt_chunk(a, c):
                act.wait_ge(pt_in_psum, 4 * a + c + 1)
                wait(act, pv_done, 4 * a)
                nc.scalar.activation(pt[:, c, :], ps_pt[c % 2][:, :], ACT.Copy).then_inc(pt_ready, 1)

            def spread_shifted(a, i, t, par, quadrants, first):
                npar, nt = next_batch(t, par)
                if first:
                    wait(act, scores_in_psum, 4 * (a + 1))
                    act.wait_ge(zeroed, 4)
                    act.wait_ge(kt_ready, group_steps(i, t))
                for j in quadrants:
                    rows, jj, block = spread(j, True)
                    nc.scalar.activation(kdiag_hi[rows, :, jj, block, :],
                                         kt[QUADRANT * j:QUADRANT * (j + 1), npar, :, N * nt:N * (nt + 1)],
                                         ACT.Copy).then_inc(kdiag_shifted_ready, 1)

            def yt_high(a):
                act.wait_ge(pv_done, 4 * (a + 1))
                wait(act, proj_in_psum, a)
                nc.scalar.activation(yt_hi[:, :, :], ps_yt[:, :].rearrange("p (c n) -> p c n", c=CHUNKS),
                                     ACT.Copy).then_inc(yt_hi_ready, 1)

            def step(i, t, par, front, middle, attention, opening):
                f, m, a = 4 * i + t, 4 * (i - 1) + t, 4 * (i - 2) + t
                if attention:
                    exp_chunk(a, 0)
                if middle:
                    if isinstance(i, int) and i == 1 and t == 0:
                        act.wait_ge(consts_loaded, 64)
                    act.wait_ge(k_in_psum, m + 1)
                    wait(act, kdiag_ready, 16 * (i - 2))
                    nc.scalar.activation(kt[:, 1 - par, t, :], ps_qk[:, :], ACT.Identity,
                                         bias=bqk[:, CHUNKS + t:CHUNKS + t + 1]).then_inc(kt_ready, 1)
                if attention:
                    exp_chunk(a, 1)
                    exp_chunk(a, 2)
                    exp_chunk(a, 3)
                    pt_chunk(a, 0)
                if has_next(i, t):
                    spread_shifted(a, i, t, par, (0, 1), True)
                if attention:
                    pt_chunk(a, 1)
                if has_next(i, t):
                    spread_shifted(a, i, t, par, (2, 3), False)
                if middle:
                    act.wait_ge(q_in_psum, m + 1)
                    wait(act, scores_in_psum, 16 * (i - 2))
                    for jj in range(2):
                        nc.scalar.activation(q_pairs[half_rows(jj), 1 - par, t, jj, :], q_bank(attention)[half_rows(jj), :], ACT.Identity,
                                             bias=bqk[half_rows(jj), t:t + 1]).then_inc(q_hi_ready, 1)
                if attention:
                    pt_chunk(a, 2)
                    pt_chunk(a, 3)
                if front:
                    act.wait_ge(ht_in_psum, f + 1)
                    wait(act, v_in_psum, 4 * (i - 1))
                    nc.scalar.activation(ht_hi[:, par, :, N * t:N * (t + 1)], ht_bank(i, t)[:, :].rearrange("p (k n) -> p k n", k=CHUNKS),
                                         ACT.Relu).then_inc(ht_hi_ready, 1)
                if attention:
                    yt_high(a)
                if middle:
                    keep_v(m, i, t, par)
                if isinstance(i, int):
                    for piece in {(0, 1): (K_FIRST,), (0, 3): (Q_FIRST, V_ALL, K_REST, Q_REST),
                                  (1, 0): (PROJ_ALL,)}.get((i, t), ()):
                        split_high(piece)

            def attention_step(i, t, par):
                a = 4 * (i - 2) + t
                exp_chunk(a, 0)
                if t > 0:
                    yt_high(a - 1)
                exp_chunk(a, 1)
                exp_chunk(a, 2)
                exp_chunk(a, 3)
                if has_next(i, t):
                    spread_shifted(a, i, t, par, (0, 1), True)
                pt_chunk(a, 0)
                if has_next(i, t):
                    spread_shifted(a, i, t, par, (2, 3), False)
                pt_chunk(a, 1)
                pt_chunk(a, 2)
                pt_chunk(a, 3)

            pipeline(act, step, attention_step)
            yt_high(BATCHES - 1)

        @block.vector
        def _(dve):
            def row_stats(i, t):
                tile, loaded, count = x_arrival(i, t)
                dve.wait_ge(loaded, count)
                nc.vector.bn_stats(stats[:, :], tile).then_inc(stats_ready, 1)

            def moments(f, slot):
                nc.vector.bn_aggr(mean_var[:, slot, :], stats[:, :]).then_inc(moments_ready, 1)
                dve.wait_ge(moments_ready, f + 1)
                nc.vector.tensor_scalar(var_eps[:, slot, :], mean_var[:, slot, 1:2], EPS, None, ALU.add).then_inc(eps_added, 1)

            def normalise(i, t):
                f, slot = 4 * i + t, t % 2
                dve.wait_ge(rstd_ready, f + 1)
                rows = x_arrival(i, t)[0]
                nc.vector.tensor_scalar(rows, rows, mean_var[:, slot, 0:1], rstd[:, slot, :],
                                        ALU.subtract, ALU.mult).then_inc(normed_ready, 1)

            def split_low(piece):
                n, columns = pieces[piece]
                dve.wait_ge(w_hi_ready, piece + 1)
                stage, high, low = weights[n]
                nc.vector.tensor_tensor(low[:, :, columns], stage[:, :, columns], high[:, :, columns].bitcast(F32),
                                        ALU.subtract).then_inc(w_ready, 1)

            def low_ht(i, t, par):
                f = 4 * i + t
                dve.wait_ge(ht_hi_ready, f + 1)
                nc.vector.scalar_tensor_tensor(out=ht_lo[:, par, :, N * t:N * (t + 1)],
                                               in0=ht_bank(i, t)[:, :].rearrange("p (k n) -> p k n", k=CHUNKS), scalar=0.0,
                                               in1=ht_hi[:, par, :, N * t:N * (t + 1)].bitcast(F32),
                                               op0=ALU.max, op1=ALU.subtract).then_inc(ht_ready, 1)

            def widen_bv():
                dve.wait_ge(consts_loaded, 64)
                wide = bv[:, :].unsqueeze(2).to_broadcast([P, CHUNKS, P])
                nc.vector.tensor_copy(yt_hi[:, :, :], wide).then_inc(bv_wide_ready, 1)
                dve.wait_ge(bv_wide_ready, 1)
                nc.vector.tensor_tensor(yt_lo[:, :, :], wide, yt_hi[:, :, :].bitcast(F32), ALU.subtract).then_inc(bv_wide_ready, 1)

            def make_out_bias():
                dve.wait_ge(bv_projected, 1)
                nc.vector.tensor_tensor(out_bias[:, :], ps_yt[:, :], out_bias[:, :], ALU.add).then_inc(out_bias_ready, 1)

            def make_mask():
                dve.wait_ge(consts_loaded, 64)
                dve.wait_ge(identity_ready, 1)
                nc.vector.tensor_tensor(mask_bias[:, :], adj_int, identity[:, :], ALU.add).then_inc(mask_step, 1)
                dve.wait_ge(mask_step, 1)
                nc.vector.tensor_scalar(mask_bias[:, :], mask_bias[:, :], 0.0, None, ALU.is_gt).then_inc(mask_step, 1)
                dve.wait_ge(mask_step, 2)
                nc.vector.tensor_scalar(mask_bias[:, :], mask_bias[:, :], 1.0, -MASKED, ALU.subtract, ALU.mult).then_inc(mask_step, 1)
                dve.wait_ge(mask_step, 3)

            def masked_max(a, c):
                dve.wait_ge(scores_in_psum, 4 * a + c + 1)
                wait(dve, pt_in_psum, 4 * a + c - 3)
                nc.vector.scalar_tensor_tensor(out=by_head(probs[:, c, :]), in0=by_head(ps_scores[c % 2][:, :]), scalar=-SCALE,
                                               in1=mask_bias[:, :].unsqueeze(1).to_broadcast([P, HPC, N]),
                                               op0=ALU.mult, op1=ALU.add).then_inc(scores_masked, 1)
                heads = slice(HPC * c, HPC * (c + 1))
                dve.wait_ge(scores_masked, 4 * a + c + 1)
                nc.vector.tensor_reduce(neg_max[:, heads], by_head(probs[:, c, :]), AX_X, ALU.min).then_inc(neg_max_ready, 1)

            def invert_sum(a, c):
                heads = slice(HPC * c, HPC * (c + 1))
                dve.wait_ge(exp_ready, 4 * a + c + 1)
                nc.vector.reciprocal(inv_sum[:, heads], row_sum[:, heads]).then_inc(inv_sum_ready, 1)

            def add_residual(b, slot):
                dve.wait_ge(proj_in_psum, b + 1)
                dve.wait_ge(res_biased, b + 1)
                nc.vector.tensor_tensor(residual[:, slot, :], ps_vo[:, :], residual[:, slot, :], ALU.add).then_inc(out_ready, 1)

            def spread_high(a, i, t, par):
                npar, nt = next_batch(t, par)
                dve.wait_ge(kt_ready, group_steps(i, t))
                wait(dve, scores_in_psum, 4 * (a + 1))
                dve.wait_ge(zeroed, 4)
                for j in range(HPC):
                    rows, jj, block = spread(j, False)
                    nc.vector.tensor_copy(kdiag_hi[rows, :, jj, block, :],
                                          kt[rows, npar, :, N * nt:N * (nt + 1)]).then_inc(kdiag_hi_ready, 1)

            def spread_low(a, t, par):
                npar, nt = next_batch(t, par)
                for j in range(HPC):
                    rows, jj, block = spread(j, False)
                    dve.wait_ge(kdiag_hi_ready, 4 * (a + 1) + j + 1)
                    nc.vector.tensor_tensor(kdiag_lo[rows, :, jj, block, :], kt[rows, npar, :, N * nt:N * (nt + 1)],
                                            kdiag_hi[rows, :, jj, block, :].bitcast(F32),
                                            ALU.subtract).then_inc(kdiag_ready, 1)

            def yt_low(a):
                dve.wait_ge(yt_hi_ready, a + 1)
                nc.vector.tensor_tensor(yt_lo[:, :, :], ps_yt[:, :].rearrange("p (c n) -> p c n", c=CHUNKS),
                                        yt_hi[:, :, :].bitcast(F32), ALU.subtract).then_inc(yt_ready, 1)

            def first_front():
                def rows(t):
                    row_stats(0, t)
                    dve.wait_ge(stats_ready, t + 1)
                    moments(t, t % 2)
                rows(0)
                rows(1)
                normalise(0, 0)
                rows(2)
                normalise(0, 1)
                rows(3)
                normalise(0, 2)
                low_ht(0, 0, 0)
                normalise(0, 3)
                low_ht(0, 1, 0)
                split_low(K_FIRST)
                low_ht(0, 2, 0)
                low_ht(0, 3, 0)
                split_low(Q_FIRST)
                split_low(V_ALL)
                split_low(K_REST)

            def step(i, t, par, front, middle, attention, opening):
                f, m, a = 4 * i + t, 4 * (i - 1) + t, 4 * (i - 2) + t
                if not middle:
                    if t == 0:
                        first_front()
                    return
                if attention:
                    masked_max(a, 0)
                if front:
                    row_stats(i, t)
                if attention:
                    masked_max(a, 1)
                if front:
                    dve.wait_ge(stats_ready, f + 1)
                if attention:
                    invert_sum(a, 0)
                if front:
                    moments(f, t % 2)
                if front and not attention:
                    normalise(i, t)
                if isinstance(i, int) and (i, t) == (1, 0):
                    split_low(Q_REST)
                if attention:
                    masked_max(a, 2)
                    invert_sum(a, 1)
                    masked_max(a, 3)
                    invert_sum(a, 2)
                if attention and not opening:
                    add_residual(a - 1, (t - 1) % 2)
                if has_next(i, t):
                    spread_high(a, i, t, par)
                if attention:
                    invert_sum(a, 3)
                if has_next(i, t):
                    spread_low(a, t, par)
                if opening:
                    make_out_bias()
                if front and attention:
                    normalise(i, t)
                for jj in range(2):
                    dve.wait_ge(q_hi_ready, 2 * m + jj + 1)
                    done = nc.vector.scalar_tensor_tensor(out=q_pairs[half_rows(1 - jj), 1 - par, t, jj, :],
                                                          in0=q_bank(attention)[half_rows(jj), :], scalar=bqk[half_rows(jj), t:t + 1],
                                                          in1=q_pairs[half_rows(jj), 1 - par, t, jj, :].bitcast(F32),
                                                          op0=ALU.add, op1=ALU.subtract)
                done.then_inc(q_ready, 1)
                if front:
                    low_ht(i, t, par)
                if isinstance(i, int) and (i, t) == (1, 0):
                    split_low(PROJ_ALL)
                if isinstance(i, int) and (i, t) == (1, 1):
                    widen_bv()
                    make_mask()
                if attention:
                    yt_low(a)

            def attention_step(i, t, par):
                a = 4 * (i - 2) + t
                masked_max(a, 0)
                masked_max(a, 1)
                invert_sum(a, 0)
                masked_max(a, 2)
                if t > 0:
                    yt_low(a - 1)
                invert_sum(a, 1)
                masked_max(a, 3)
                invert_sum(a, 2)
                if has_next(i, t):
                    spread_high(a, i, t, par)
                invert_sum(a, 3)
                if has_next(i, t):
                    spread_low(a, t, par)
                add_residual(a - 1, (t - 1) % 2)

            pipeline(dve, step, attention_step)
            yt_low(BATCHES - 1)
            add_residual(BATCHES - 1, (BATCHES - 1) % 2)

        @block.tensor
        def _(pe):
            pe.wait_ge(identity_ready, 1)

            def three_passes(out_tile, stationary, moving, ks, first, last):
                (s_hi, s_lo), (m_hi, m_lo) = stationary, moving
                for k in ks:
                    for n, (s, m) in enumerate(((s_hi, m_hi), (s_hi, m_lo), (s_lo, m_hi))):
                        done = nc.tensor.matmul(out_tile, s(k), m(k), start=(first and k == ks[0] and n == 0),
                                                stop=(last and k == ks[-1] and n == 2))
                return done

            def projection(out_tile, stationary, moving, half):
                ks = list(range(CHUNKS // 2)) if half == 0 else list(range(CHUNKS // 2, CHUNKS))
                return three_passes(out_tile, stationary, moving, ks, half == 0, half == 1)

            def parts(hi, lo, at):
                return (lambda k: at(hi, k)), (lambda k: at(lo, k))

            def qk_half(bank, i, t, par, offset, half):
                return projection(bank[:, :],
                                  parts(wqkv_hi, wqkv_lo, lambda w, k: w[:, k, offset + P * t:offset + P * (t + 1)]),
                                  parts(ht_hi, ht_lo, lambda h, k: h[:, 1 - par, k, :]), half)

            def k_half(i, t, par, half, attention, opening):
                m = 4 * (i - 1) + t
                if half == 0:
                    if isinstance(i, int) and i == 1 and t < 2:
                        pe.wait_ge(w_ready, (K_FIRST, K_REST)[t] + 1)
                    if t == 0:
                        pe.wait_ge(ht_ready, 4 * i)
                    if attention and not opening:
                        pe.wait_ge(q_ready, m)
                    else:
                        wait(pe, kt_ready, m)
                done = qk_half(ps_qk, i, t, par, E, half)
                if half == 1:
                    done.then_inc(k_in_psum, 1)

            def q_half(i, t, par, half, attention):
                m = 4 * (i - 1) + t
                if half == 0:
                    if isinstance(i, int) and i == 1 and t < 2:
                        pe.wait_ge(w_ready, (Q_FIRST, Q_REST)[t] + 1)
                    if attention:
                        pe.wait_ge(kt_ready, m + 1)
                    else:
                        wait(pe, q_ready, m)
                done = qk_half(q_bank(attention), i, t, par, 0, half)
                if half == 1:
                    done.then_inc(q_in_psum, 1)

            def v_half(i, t, par, half, after_projection):
                if isinstance(i, int) and i == 1 and t == 0 and half == 0:
                    pe.wait_ge(w_ready, V_ALL + 1)
                if half == 0 and after_projection:
                    pe.wait_ge(out_ready, 4 * (i - 2) + t)
                elif half == 0:
                    wait(pe, v_ready, 4 * (i - 1) + t)
                done = projection(ps_vo[:, :],
                                  parts(ht_hi, ht_lo, lambda h, k: h[:, 1 - par, k, N * t:N * (t + 1)]),
                                  parts(wqkv_hi, wqkv_lo, lambda w, k: w[:, k, 2 * E:3 * E]), half)
                if half == 1:
                    done.then_inc(v_in_psum, 1)

            def proj_half(b, vs, half):
                if half == 0:
                    pe.wait_ge(yt_ready, b + 1)
                    pe.wait_ge(v_ready, vs)
                done = projection(ps_vo[:, :], parts(yt_hi, yt_lo, lambda y, k: y[:, k, :]),
                                  parts(wproj_hi, wproj_lo, lambda w, k: w[:, k, :]), half)
                if half == 1:
                    done.then_inc(proj_in_psum, 1)

            def scores(i, t, par, c):
                a = 4 * (i - 2) + t
                if c == 0:
                    pe.wait_ge(kdiag_ready, 4 * (a + 1))
                    pe.wait_ge(kdiag_shifted_ready, 4 * (a + 1))
                    if t == 0:
                        pe.wait_ge(q_ready, 4 * (i - 1))
                wait(pe, scores_masked, 4 * a + c - 1)
                for jj in range(2):
                    q_tile = q_pairs[:, par, c, jj, N * t:N * (t + 1)]
                    pair = ps_scores[c % 2][:, 2 * N * jj:2 * N * (jj + 1)]
                    nc.tensor.matmul(pair, q_tile, kdiag_hi[:, c, jj, :, :], start=True, stop=False)
                    last = nc.tensor.matmul(pair, q_tile, kdiag_lo[:, c, jj, :, :], start=False, stop=True)
                last.then_inc(scores_in_psum, 1)

            def transpose_probs(a, c):
                pe.wait_ge(probs_ready, 4 * a + c + 1)
                wait(pe, pt_ready, 4 * a + c - 1)
                for j in range(HPC):
                    last = nc.tensor.transpose(ps_pt[c % 2][:, N * j:N * (j + 1)], probs[:, c, N * j:N * (j + 1)], identity[:, :])
                last.then_inc(pt_in_psum, 1)

            def pv(i, t, par, c):
                a = 4 * (i - 2) + t
                if c == 0:
                    if isinstance(a, int) and a == 0:
                        pe.wait_ge(out_bias_ready, 1)
                    pe.wait_ge(v_ready, a + 1)
                    wait(pe, yt_ready, a)
                pe.wait_ge(pt_ready, 4 * a + c + 1)
                for j in range(HPC):
                    h = HPC * c + j
                    last = nc.tensor.matmul(ps_yt[QUADRANT * j:QUADRANT * (j + 1), N * c:N * (c + 1)],
                                            v[:, GROUP * par + t, DH * h:DH * (h + 1)],
                                            pt[:, c, N * j:N * (j + 1)], start=True, stop=True)
                last.then_inc(pv_done, 1)

            def transpose_rows(i, t):
                f = 4 * i + t
                pe.wait_ge(normed_ready, f + 1)
                if not (isinstance(i, int) and i == 0):
                    pe.wait_ge(ht_ready, f)
                for k in range(CHUNKS):
                    last = nc.tensor.transpose(ht_bank(i, t)[:, N * k:N * (k + 1)], x_arrival(i, t)[0][:, P * k:P * (k + 1)], identity[:, :])
                last.then_inc(ht_in_psum, 1)

            def project_bv():
                pe.wait_ge(w_ready, PROJ_ALL + 1)
                pe.wait_ge(bv_wide_ready, 2)
                last = three_passes(ps_yt[:, :], parts(yt_hi, yt_lo, lambda y, k: y[:, k, :]),
                                    parts(wproj_hi, wproj_lo, lambda w, k: w[:, k, :]), list(range(CHUNKS)), True, True)
                last.then_inc(bv_projected, 1)

            def step(i, t, par, front, middle, attention, opening):
                a, v_steps = 4 * (i - 2) + t, 4 * (i - 1) + t
                if not attention:
                    if middle:
                        k_half(i, t, par, 0, attention, opening)
                        k_half(i, t, par, 1, attention, opening)
                        q_half(i, t, par, 0, attention)
                        q_half(i, t, par, 1, attention)
                    if middle and t == GROUP - 1:
                        transpose_rows(i, t)
                    if middle:
                        v_half(i, t, par, 0, False)
                        v_half(i, t, par, 1, False)
                    if not middle or t < GROUP - 1:
                        transpose_rows(i, t)
                    return
                scores(i, t, par, 0)
                k_half(i, t, par, 0, attention, opening)
                scores(i, t, par, 1)
                k_half(i, t, par, 1, attention, opening)
                scores(i, t, par, 2)
                if not opening:
                    proj_half(a - 1, v_steps, 0)
                scores(i, t, par, 3)
                if not opening:
                    proj_half(a - 1, v_steps, 1)
                else:
                    project_bv()
                q_half(i, t, par, 0, attention)
                transpose_probs(a, 0)
                q_half(i, t, par, 1, attention)
                transpose_probs(a, 1)
                v_half(i, t, par, 0, not opening)
                transpose_probs(a, 2)
                transpose_probs(a, 3)
                v_half(i, t, par, 1, not opening)
                if front:
                    transpose_rows(i, t)
                pv(i, t, par, 0)
                pv(i, t, par, 1)
                pv(i, t, par, 2)
                pv(i, t, par, 3)

            def attention_step(i, t, par):
                a = 4 * (i - 2) + t
                scores(i, t, par, 0)
                if t > 0:
                    pv(i, t - 1, par, 1)
                    transpose_probs(a - 1, 3)
                scores(i, t, par, 1)
                if t > 0:
                    pv(i, t - 1, par, 2)
                    pv(i, t - 1, par, 3)
                scores(i, t, par, 2)
                scores(i, t, par, 3)
                transpose_probs(a, 0)
                proj_half(a - 1, BATCHES, 0)
                transpose_probs(a, 1)
                proj_half(a - 1, BATCHES, 1)
                transpose_probs(a, 2)
                pv(i, t, par, 0)
                if t == GROUP - 1:
                    pv(i, t, par, 1)
                    transpose_probs(a, 3)
                    pv(i, t, par, 2)
                    pv(i, t, par, 3)

            pipeline(pe, step, attention_step)
            proj_half(BATCHES - 1, BATCHES, 0)
            proj_half(BATCHES - 1, BATCHES, 1)


def kernel(x, adj, L0_gnn_Wqkv, L0_gnn_bqkv, L0_gnn_Wproj, L0_gnn_bproj):
    import numpy as np
    import concourse.bacc as bacc
    from concourse.bass_utils import run_bass_kernel_spmd

    e = L0_gnn_Wproj.shape[0]
    bqkv = np.asarray(L0_gnn_bqkv)
    arrays = {
        "x": np.ascontiguousarray(x),
        "adj": np.ascontiguousarray(adj),
        "w_qkv": np.ascontiguousarray(L0_gnn_Wqkv),
        "b_qk_columns": np.ascontiguousarray(bqkv[:2 * e].reshape(2 * e // P, P).T),
        "b_v_columns": np.ascontiguousarray(bqkv[2 * e:].reshape(e // P, P).T),
        "w_proj": np.ascontiguousarray(L0_gnn_Wproj),
        "b_proj": np.ascontiguousarray(np.asarray(L0_gnn_bproj).reshape(1, e)),
    }
    nc = bacc.Bacc("TRN2", target_bir_lowering=False, num_devices=1)
    args = [nc.dram_tensor(f"in_{name}", a.shape, mybir.dt.from_np(a.dtype), kind="ExternalInput").ap()
            for name, a in arrays.items()]
    out = nc.dram_tensor("out_0", arrays["x"].shape, F32, kind="ExternalOutput").ap()
    graph_attention_block(nc, *args, out)
    r = run_bass_kernel_spmd(nc, [{f"in_{name}": a for name, a in arrays.items()}], core_ids=[0])
    return r.results[0]["out_0"]
```
